# Optimizing a Trainium2 kernel written in Bass

```python
import numpy as np
import jax
import jax.numpy as jnp

def _softmax(x, axis=-1):
    return jax.nn.softmax(x, axis=axis)

def _gelu(x):
    return jax.nn.gelu(x, approximate=True)

def _silu(x):
    return jax.nn.silu(x)

def _sigmoid(x):
    return jax.nn.sigmoid(x)

def _layernorm(x, axis=-1, eps=1e-05):
    m = jnp.mean(x, axis=axis, keepdims=True)
    v = jnp.var(x, axis=axis, keepdims=True)
    return (x - m) / jnp.sqrt(v + eps)

def _scatter_add(tgt, idx, src, axis=0):
    return tgt.at[idx].add(src)

def _segment_sum(src, seg, n):
    return jax.ops.segment_sum(src, seg, n)
kernel_name = 'mk_conv_seq_d2_conv_nchw256_r2_d65dff'

def setup_inputs(seed: int=0):
    np.random.seed(seed)
    _w = jnp.asarray

    def _rec_inputs():
        import jax
        import jax.numpy as jnp
        _gk = jax.random.key(seed)
        x = -0.0002928 + 1 * jax.random.normal(jax.random.fold_in(_gk, 1), (16, 128, 32, 32), jnp.float32)
        return x
    x = _rec_inputs()

    def _L0_conv_setup():
        import jax, jax.numpy as jnp
        import numpy as np
        from math import sqrt
        DIM = 128
        HEADS = 4
        GROUPS = min(DIM // 4, 32)
        EPS = 1e-06

        def _group_norm(x, scale, bias):
            B, C, H, W = x.shape
            xg = x.reshape(B, GROUPS, C // GROUPS, H, W)
            mean = xg.mean(axis=(2, 3, 4), keepdims=True)
            var = xg.var(axis=(2, 3, 4), keepdims=True)
            xg = (xg - mean) * jax.lax.rsqrt(var + EPS)
            x = xg.reshape(B, C, H, W)
            return x * scale[None, :, None, None] + bias[None, :, None, None]

        def _lin_ch(x, W, b):
            return jnp.einsum('bchw,cd->bdhw', x, W) + b[None, :, None, None]
        key = jax.random.key(seed)
        ks = jax.random.split(key, 10)
        B, C, H, W = (16, DIM, 32, 32)
        x = jax.random.normal(ks[0], (B, C, H, W), dtype=jnp.float32)
        s = 1.0 / sqrt(C)
        inp = {'x': x, 'gn_scale': jnp.ones((C,), jnp.float32), 'gn_bias': jnp.zeros((C,), jnp.float32), 'Wq': jax.random.normal(ks[1], (C, C), jnp.float32) * s, 'bq': jnp.zeros((C,), jnp.float32), 'Wk': jax.random.normal(ks[2], (C, C), jnp.float32) * s, 'bk': jnp.zeros((C,), jnp.float32), 'Wv': jax.random.normal(ks[3], (C, C), jnp.float32) * s, 'bv': jnp.zeros((C,), jnp.float32), 'Wp': jax.random.normal(ks[4], (C, C), jnp.float32) * s, 'bp': jnp.zeros((C,), jnp.float32)}
        return inp
    _L0_conv_all = _L0_conv_setup()
    _L0_conv_in = {k: v for k, v in _L0_conv_all.items() if k in ('gn_scale', 'gn_bias', 'Wq', 'bq', 'Wk', 'bk', 'Wv', 'bv', 'Wp', 'bp')}
    del _L0_conv_all

    def _L1_conv_setup():
        import jax, jax.numpy as jnp
        import numpy as np
        NUM_GROUPS = 8
        EPS = 1e-05

        def _group_norm(x, w, b):
            B, C, H, W = x.shape
            g = NUM_GROUPS
            xg = x.reshape(B, g, C // g, H, W)
            mean = jnp.mean(xg, axis=(2, 3, 4), keepdims=True)
            var = jnp.var(xg, axis=(2, 3, 4), keepdims=True)
            xn = (xg - mean) * jax.lax.rsqrt(var + EPS)
            xn = xn.reshape(B, C, H, W)
            return xn * w[None, :, None, None] + b[None, :, None, None]
        key = jax.random.key(seed)
        ks = jax.random.split(key, 4)
        B, C, H, W = (4, 128, 32, 32)
        x = jax.random.normal(ks[0], (B, C, H, W), dtype=jnp.float32)
        gn_w = jnp.ones((C,), dtype=jnp.float32)
        gn_b = jnp.zeros((C,), dtype=jnp.float32)
        qkv_w = jax.random.normal(ks[1], (3 * C, C), dtype=jnp.float32) * (1.0 / np.sqrt(C))
        qkv_b = jnp.zeros((3 * C,), dtype=jnp.float32)
        proj_w = jax.random.normal(ks[2], (C, C), dtype=jnp.float32) * (1.0 / np.sqrt(C))
        proj_b = jnp.zeros((C,), dtype=jnp.float32)
        return {'x': x, 'gn_w': gn_w, 'gn_b': gn_b, 'qkv_w': qkv_w, 'qkv_b': qkv_b, 'proj_w': proj_w, 'proj_b': proj_b}
    _L1_conv_all = _L1_conv_setup()
    _L1_conv_in = {k: v for k, v in _L1_conv_all.items() if k in ('gn_w', 'gn_b', 'qkv_w', 'qkv_b', 'proj_w', 'proj_b')}
    del _L1_conv_all
    return {'x': x, 'L0_conv_gn_scale': _L0_conv_in['gn_scale'], 'L0_conv_gn_bias': _L0_conv_in['gn_bias'], 'L0_conv_Wq': _L0_conv_in['Wq'], 'L0_conv_bq': _L0_conv_in['bq'], 'L0_conv_Wk': _L0_conv_in['Wk'], 'L0_conv_bk': _L0_conv_in['bk'], 'L0_conv_Wv': _L0_conv_in['Wv'], 'L0_conv_bv': _L0_conv_in['bv'], 'L0_conv_Wp': _L0_conv_in['Wp'], 'L0_conv_bp': _L0_conv_in['bp'], 'L1_conv_gn_w': _L1_conv_in['gn_w'], 'L1_conv_gn_b': _L1_conv_in['gn_b'], 'L1_conv_qkv_w': _L1_conv_in['qkv_w'], 'L1_conv_qkv_b': _L1_conv_in['qkv_b'], 'L1_conv_proj_w': _L1_conv_in['proj_w'], 'L1_conv_proj_b': _L1_conv_in['proj_b']}

def reference(x, L0_conv_gn_scale, L0_conv_gn_bias, L0_conv_Wq, L0_conv_bq, L0_conv_Wk, L0_conv_bk, L0_conv_Wv, L0_conv_bv, L0_conv_Wp, L0_conv_bp, L1_conv_gn_w, L1_conv_gn_b, L1_conv_qkv_w, L1_conv_qkv_b, L1_conv_proj_w, L1_conv_proj_b):
    import jax
    import jax.numpy as jnp

    def _L0_conv_ref(x, gn_scale, gn_bias, Wq, bq, Wk, bk, Wv, bv, Wp, bp):
        import jax, jax.numpy as jnp
        import numpy as np
        from math import sqrt
        DIM = 128
        HEADS = 4
        GROUPS = min(DIM // 4, 32)
        EPS = 1e-06

        def _group_norm(x, scale, bias):
            B, C, H, W = x.shape
            xg = x.reshape(B, GROUPS, C // GROUPS, H, W)
            mean = xg.mean(axis=(2, 3, 4), keepdims=True)
            var = xg.var(axis=(2, 3, 4), keepdims=True)
            xg = (xg - mean) * jax.lax.rsqrt(var + EPS)
            x = xg.reshape(B, C, H, W)
            return x * scale[None, :, None, None] + bias[None, :, None, None]

        def _lin_ch(x, W, b):
            return jnp.einsum('bchw,cd->bdhw', x, W) + b[None, :, None, None]
        B, C, H, W = x.shape
        dh = C // HEADS
        _x = _group_norm(x, gn_scale, gn_bias)
        q = _lin_ch(_x, Wq, bq).reshape(B, HEADS, dh, H, W)
        k = _lin_ch(_x, Wk, bk).reshape(B, HEADS, dh, H, W)
        v = _lin_ch(_x, Wv, bv).reshape(B, HEADS, dh, H, W)
        scores = jnp.einsum('bhdxy,bhdij->bhxyij', q, k) / sqrt(C)
        scores = scores.reshape(B, HEADS, H, W, H * W)
        weights = jax.nn.softmax(scores, axis=-1).reshape(B, HEADS, H, W, H, W)
        h = jnp.einsum('bhxyij,bhdij->bhdxy', weights, v).reshape(B, C, H, W)
        h = _lin_ch(h, Wp, bp)
        ret = (x + h) / sqrt(2.0)
        return ret

    def _L1_conv_ref(x, gn_w, gn_b, qkv_w, qkv_b, proj_w, proj_b):
        import jax, jax.numpy as jnp
        import numpy as np
        NUM_GROUPS = 8
        EPS = 1e-05

        def _group_norm(x, w, b):
            B, C, H, W = x.shape
            g = NUM_GROUPS
            xg = x.reshape(B, g, C // g, H, W)
            mean = jnp.mean(xg, axis=(2, 3, 4), keepdims=True)
            var = jnp.var(xg, axis=(2, 3, 4), keepdims=True)
            xn = (xg - mean) * jax.lax.rsqrt(var + EPS)
            xn = xn.reshape(B, C, H, W)
            return xn * w[None, :, None, None] + b[None, :, None, None]
        B, C, H, W = x.shape
        N = H * W
        h = _group_norm(x, gn_w, gn_b)
        h_flat = h.reshape(B, C, N).transpose(0, 2, 1)
        qkv = jnp.einsum('bnc,oc->bno', h_flat, qkv_w) + qkv_b
        q, k, v = jnp.split(qkv, 3, axis=-1)
        scale = 1.0 / jnp.sqrt(jnp.asarray(C, dtype=x.dtype))
        scores = jnp.einsum('bnc,bmc->bnm', q, k) * scale
        attn = jax.nn.softmax(scores, axis=-1)
        out = jnp.einsum('bnm,bmc->bnc', attn, v)
        out = jnp.einsum('bnc,oc->bno', out, proj_w) + proj_b
        out = out.transpose(0, 2, 1).reshape(B, C, H, W)
        return out + x

    def _gn(v, G=32, eps=1e-05):
        B_, C_, H_, W_ = v.shape
        g = v.reshape(B_, G, C_ // G, H_, W_)
        m = jnp.mean(g, axis=(2, 3, 4), keepdims=True)
        s = jnp.var(g, axis=(2, 3, 4), keepdims=True)
        return ((g - m) / jnp.sqrt(s + eps)).reshape(v.shape)

    def _ln_c(v, eps=1e-06):
        m = jnp.mean(v, axis=1, keepdims=True)
        s = jnp.var(v, axis=1, keepdims=True)
        return (v - m) / jnp.sqrt(s + eps)

    def _ln_t(v, eps=1e-05):
        m = jnp.mean(v, axis=-1, keepdims=True)
        s = jnp.var(v, axis=-1, keepdims=True)
        return (v - m) / jnp.sqrt(s + eps)

    def _to_tokens(v):
        B_, C_, H_, W_ = v.shape
        return v.reshape(B_, C_, H_ * W_).transpose(0, 2, 1)

    def _from_tokens(t, like):
        B_, C_, H_, W_ = like.shape
        return t.transpose(0, 2, 1).reshape(B_, C_, H_, W_)
    x = _L0_conv_ref(x, L0_conv_gn_scale, L0_conv_gn_bias, L0_conv_Wq, L0_conv_bq, L0_conv_Wk, L0_conv_bk, L0_conv_Wv, L0_conv_bv, L0_conv_Wp, L0_conv_bp)
    x = _L1_conv_ref(x, L1_conv_gn_w, L1_conv_gn_b, L1_conv_qkv_w, L1_conv_qkv_b, L1_conv_proj_w, L1_conv_proj_b)
    return x

_drawn_inputs = setup_inputs


def setup_inputs(seed=0):
    import zlib

    import numpy as np

    out = dict(_drawn_inputs(seed))
    spreads = {'L0_conv_gn_scale': (1.0, 0.6),
     'L0_conv_gn_bias': (0.0, 0.1),
     'L0_conv_bq': (0.0, 0.8),
     'L0_conv_bk': (0.0, 0.8),
     'L0_conv_bv': (0.0, 0.1),
     'L0_conv_bp': (0.0, 0.1),
     'L1_conv_gn_w': (1.0, 0.2),
     'L1_conv_gn_b': (0.0, 0.1),
     'L1_conv_qkv_b': (0.0, 0.1),
     'L1_conv_proj_b': (0.0, 0.1)}
    factors = {}
    for name, (base, spread) in spreads.items():
        noise = np.random.default_rng([zlib.crc32(name.encode()), seed]).standard_normal(out[name].shape)
        drawn = base * np.exp(spread * noise) if base else spread * noise
        out[name] = jnp.asarray(drawn.astype(out[name].dtype))
    for name, factor in factors.items():
        out[name] = (out[name] * factor).astype(out[name].dtype)
    return out
```

```python
from contextlib import ExitStack
import math

import concourse.bass as bass
from concourse import mybir

F32 = mybir.dt.float32
F32R = mybir.dt.float32r
ALU = mybir.AluOpType
ACT = mybir.ActivationFunctionType
AX = mybir.AxisListType

C = 128
N = 1024
HALF = 512
KT = N // C
HEADS = 4
DH = C // HEADS
SPLIT = 3 * DH
SHIFT = 2
NVEC = 12
P_RING = 10
SCALE = 1.0 / math.sqrt(C)
EPS = (1e-6, 1e-5)

WQ, WK, WV, WP = range(4)
GAMMA, BETA, BQ, BK, BV, BP = range(6)
MAXES_IN_X = 20


def background_x(i, images):
    own, nxt, last = i - 1, i + 1, i - 2
    has_own = not isinstance(i, int) or 0 <= own < images
    has_last = not isinstance(i, int) or 0 <= last < images
    has_next = not isinstance(i, int) or nxt < images
    steps = []
    if has_next:
        steps += [("stats0", nxt, 0)]
    if has_last:
        steps += [("sums1", last, 0), ("sums1", last, 1)]
    if has_own:
        steps += [("q1", own, 0), ("q1", own, 1), ("k1", own, 0), ("k1", own, 1)]
    if has_next:
        steps += [("mean0", nxt, 0)]
    if has_own:
        steps += [("v1", own, 0), ("v1", own, 1)]
    if has_next:
        steps += [("var0", nxt, 0)]
    if has_own:
        steps += [("max1", own, n) for n in range(4)]
    if has_next:
        steps += [("norm0", nxt, 0), ("q0", nxt, 0), ("q0", nxt, 1), ("k0", nxt, 0), ("k0", nxt, 1)]
    if has_last:
        steps += [("recip1", last, 0)]
    if has_own:
        steps += [("max1", own, n) for n in range(4, 8)]
    if has_next:
        steps += [("v0", nxt, 0), ("v0", nxt, 1)]
    if has_own:
        steps += [("max1", own, n) for n in range(8, 16)]
    if has_last:
        steps += [("scale1", last, 0)]
    if has_own:
        steps += [("gather1", own, 0), ("shift1", own, 0)]
    if has_last:
        steps += [("proj1", last, 0), ("proj1", last, 1)]
    if has_next:
        steps += [("max0", nxt, n) for n in range(MAXES_IN_X)]
    return steps


def background_y(i, images):
    nxt = i + 1
    has_this = not isinstance(i, int) or i < images
    has_next = not isinstance(i, int) or nxt < images
    count = MAXES_IN_X
    steps = []

    def maxes(n):
        nonlocal count
        found = [("max0", nxt, count + m) for m in range(n)] if has_next else []
        count += n
        return found

    total = 2 * KT * HEADS
    steps += maxes(6)
    if has_this:
        steps += [("sums0", i, 0), ("sums0", i, 1)]
    steps += maxes(12)
    if has_this:
        steps += [("recip0", i, 0)]
    steps += maxes(6)
    if has_this:
        steps += [("scale0", i, 0)]
    steps += maxes(1)
    if has_this:
        steps += [("proj0", i, 0), ("proj0", i, 1), ("stats1", i, 0)]
    steps += maxes(2)
    if has_this:
        steps += [("mean1", i, 0)]
    steps += maxes(2)
    if has_this:
        steps += [("var1", i, 0)]
    steps += maxes(3)
    if has_this:
        steps += [("norm1", i, 0)]
    steps += maxes(total - count)
    if has_next:
        steps += [("gather0", nxt, 0), ("shift0", nxt, 0)]
    return steps


def background_start():
    return ([("stats0", 0, 0), ("mean0", 0, 0), ("var0", 0, 0), ("norm0", 0, 0),
             ("q0", 0, 0), ("q0", 0, 1), ("k0", 0, 0), ("k0", 0, 1), ("v0", 0, 0), ("v0", 0, 1)]
            + [("max0", 0, n) for n in range(2 * KT * HEADS)] + [("gather0", 0, 0), ("shift0", 0, 0)])


WORK = ("sums", "q", "k", "v", "mean", "var", "max", "shift", "proj")


def uses_work(step):
    return step[0][:-1] in WORK


def work_count(steps):
    return sum(map(uses_work, steps))


def bass_two_attention_blocks(nc, x, weights, vectors, constants, out):
    images = x.shape[0]
    x_dram = x.rearrange("b c h w -> b c (h w)")
    out_dram = out.rearrange("b c h w -> b c (h w)")

    per_body = work_count(background_x(5, images)) + work_count(background_y(5, images))

    def work_before_x(i):
        if isinstance(i, int) and i < 2:
            at = work_count(background_start())
            for n in range(i):
                at += work_count(background_x(n, images)) + work_count(background_y(n, images))
            return at
        if isinstance(i, int) and i >= images:
            at = work_before_x(images - 1)
            for n in range(images - 1, i):
                at += work_count(background_x(n, images)) + work_count(background_y(n, images))
            return at
        return work_before_x(1) + work_count(background_x(1, images)) \
            + work_count(background_y(1, images)) + (i - 2) * per_body

    def work_before_y(i, xs):
        return work_before_x(i) + work_count(xs)

    def before_x(i, x_count, y_count):
        return 0 if isinstance(i, int) and i == 0 else (x_count + y_count) * i - y_count

    def before_y(i, x_count, y_count):
        if isinstance(i, int) and i >= images:
            return before_x(i, x_count, y_count)
        return before_x(i, x_count, y_count) + x_count

    def scores_before(i, y):
        return (before_y if y else before_x)(i, KT * HEADS, KT)

    def ring_before(i, y):
        return (before_y if y else before_x)(i, (KT - 1) * HEADS, KT - 1)

    def pv_before(i, y):
        return (before_y if y else before_x)(i, KT, KT)

    POOL_HEADS = HEADS - 1

    def pool_adds_before(i, y):
        return (before_y if y else before_x)(i, (KT - 1) * POOL_HEADS, KT - 1)

    def saved_before(i, y):
        return (before_y if y else before_x)(i, 1, 1)

    def ring_slot(i, parity, y, n):
        j = i if isinstance(i, int) else 2 + parity
        return (ring_before(j, y) + n) % P_RING

    with ExitStack() as ctx:
        def sb(name, shape, dt=F32):
            return ctx.enter_context(nc.sbuf_tensor(name, shape, dt))

        def ps(name, shape, dt=F32):
            return ctx.enter_context(nc.psum_tensor(name, shape, dt))

        def sem(name):
            return ctx.enter_context(nc.semaphore(name))

        wts = sb("wts", [C, 8, C])
        vecs = sb("vecs", [C, NVEC])
        consts = sb("consts", [C, 3, C])
        ones = sb("ones", [C, C], F32R)
        minus_half = sb("minus_half", [C, 1])
        xin = sb("xin", [C, 2, N])
        x1 = sb("x1", [C, 2, N])
        xh = sb("xh", [C, N])
        part = [sb(n, [C, N], F32R) for n in ("q_hi", "q_lo", "k_hi", "k_lo")]
        qs = [sb(f"q_stack{p}", [C, HEADS, N], F32R) for p in range(2)]
        ks = [sb(f"k_stack{p}", [C, HEADS, N], F32R) for p in range(2)]
        part1 = [sb(n, [C, N], F32R) for n in ("q1_hi", "q1_lo", "k1_hi", "k1_lo")]
        shift1 = sb("shift1", [C, N], F32R)
        v0 = sb("v0", [C, 2, KT, C])
        v1 = sb("v1", [C, KT, C])
        probs = sb("probs", [C, P_RING, N])
        sum0 = sb("sum0", [C, HEADS, N])
        sum1 = part[0][:, :].bitcast(F32)
        mix = sb("mix", [C, N])
        rb = sb("rb", [C, N])
        compact = [sb(f"compact{b}", [C, h * KT]) for b, h in ((0, HEADS), (1, 1))]
        halfmax = [sb(f"halfmax{b}", [C, h * KT, 2]) for b, h in ((0, HEADS), (1, 1))]
        rowmax = [sb(f"rowmax{b}", [C, h * KT]) for b, h in ((0, HEADS), (1, 1))]
        neg = [sb(n, [HEADS * KT, C], F32R) for n in ("neg_hi", "neg_lo")]
        stats = [sb(f"stats{b}", [C, 2, 6]) for b in range(2)]
        mv = [sb(f"mv{b}", [C, 2]) for b in range(2)]
        gn = [sb(f"gn{b}", [C, 8]) for b in range(2)]
        proj_bias = sb("proj_bias", [C, 2])
        DIFF, GMEAN, VARIN, VAREPS, RSTD, GAIN, MG, OFFSET = range(8)

        sums_dram = [nc.dram_tensor(f"sums_dram{b}", (h, N), F32).ap() for b, h in ((0, HEADS), (1, 1))]
        recip_dram = [nc.dram_tensor(f"recip_dram{b}", (h, N), F32).ap() for b, h in ((0, HEADS), (1, 1))]

        score = [ps(f"score{n}", [C, N]) for n in range(2)]
        acc = ps("acc", [C, N])
        work = [ps(f"work{n}", [C, HALF]) for n in range(2)]

        const_loaded = sem("const_loaded")
        pool_ready = sem("pool_ready")
        bias_ready = sem("bias_ready")
        x_loaded = sem("x_loaded")
        work_full = sem("work_full")
        work_free = sem("work_free")
        hi_done = [sem(f"hi_done{b}") for b in range(2)]
        neg_done = [sem(f"neg_done{b}") for b in range(2)]
        dve_setup = sem("dve_setup")
        gn_chain = [sem(f"gn_chain{b}") for b in range(2)]
        GN_CHAIN = 10
        rstd_done = [sem(f"rstd_done{b}") for b in range(2)]
        stacked = sem("stacked")
        STACK_DMAS = 6 * HEADS
        rowmax_done = [sem(f"rowmax_done{b}") for b in range(2)]
        shift_loaded = [sem(f"shift_loaded{b}") for b in range(2)]
        score_full = sem("score_full")
        probs_done = sem("probs_done")
        pv_done = sem("pv_done")
        pool_added = sem("pool_added")
        dve_added = sem("dve_added")
        saved = sem("saved")
        sums_out = [sem(f"sums_out{b}") for b in range(2)]
        sums_in = [sem(f"sums_in{b}") for b in range(2)]
        recip_done = [sem(f"recip_done{b}") for b in range(2)]
        recip_out = [sem(f"recip_out{b}") for b in range(2)]
        rb_loaded = [sem(f"rb_loaded{b}") for b in range(2)]
        scaled = [sem(f"scaled{b}") for b in range(2)]
        x1_done = sem("x1_done")
        stored = sem("stored")

        def w(b, which):
            return wts[:, 4 * b + which, :]

        def vec(b, which):
            return vecs[:, 6 * b + which:6 * b + which + 1]

        identity = consts[:, 0, :]

        def halves(h):
            return slice(HALF * h, HALF * (h + 1))

        def tile(t):
            return slice(C * t, C * (t + 1))

        def head(h):
            return slice(DH * h, DH * (h + 1))

        def position(steps, base, name, arg):
            n = 0
            for s in steps:
                if s[0] == name and s[2] == arg:
                    return base + n
                n += uses_work(s)
            return None

        def x_position(i, name, arg):
            return position(background_x(i, images), work_before_x(i), name, arg)

        def y_position(i, name, arg):
            return position(background_y(i, images), work_before_y(i, background_x(i, images)), name, arg)

        def work_parity(i, parity, y):
            j = i if isinstance(i, int) else 2 + parity
            return (work_before_y(j, background_x(j, images)) if y else work_before_x(j)) % 2

        def spread(steps, gaps):
            cut = [len(steps) * g // gaps for g in range(gaps + 1)]
            return [steps[a:b] for a, b in zip(cut, cut[1:])]

        def gaps_x(i):
            return spread(background_x(i, images), KT * HEADS)

        Y_FILLED = 14

        def gaps_y(i):
            return spread(background_y(i, images), Y_FILLED) + [[]] * (2 * KT - Y_FILLED)

        def parity_of(s, parity):
            name, b = s[0][:-1], int(s[0][-1])
            same = name in ("sums", "recip", "scale", "proj") or (b == 1 and name in ("stats", "mean", "var", "norm"))
            return parity if same else 1 - parity

        def bodies(engine, body):
            body(0, 0)
            body(1, 1)
            with engine.Fori(1, images // 2 - 1) as pair:
                body(2 * pair, 0)
                body(2 * pair + 1, 1)
            body(images - 2, 0)
            body(images - 1, 1)

        block = ctx.enter_context(nc.Block())

        @block.sync
        def _(sp):
            sp.dma_start(xin[:, 0, :], x_dram[0]).then_inc(x_loaded, 16)
            sp.dma_start(wts[:, :, :], weights).then_inc(const_loaded, 16)
            sp.dma_start(vecs[:, :], vectors).then_inc(const_loaded, 16)
            sp.dma_start(consts[:, :, :], constants).then_inc(const_loaded, 16)
            sp.dma_start(xin[:, 1, :], x_dram[1]).then_inc(x_loaded, 16)

            def stack(img, par, which, evacuated):
                sp.wait_ge(work_free, evacuated + 1)
                hi, lo = part[2 * which], part[2 * which + 1]
                dst = (qs, ks)[which][par]
                for group, src in enumerate((hi, lo, hi) if which == 0 else (hi, hi, lo)):
                    for h in range(HEADS):
                        sp.dma_start(dst[DH * group:DH * (group + 1), h, :].bitcast(F32),
                                     src[head(h), :].bitcast(F32)).then_inc(stacked, 16)

            def step(s, par, at):
                name, img, arg = s
                b = int(name[-1])
                name = name[:-1]
                if name == "q" and b == 0 and arg == 1:
                    stack(img, par, 0, at)
                elif name == "k" and b == 0 and arg == 1:
                    stack(img, par, 1, at)
                elif name == "shift":
                    sp.wait_ge(work_free, at + 1)
                    if b == 0:
                        dst = qs[par]
                        rows = [dst[SPLIT + n:SPLIT + n + 1, :, :].rearrange("p h (t n) -> p (h t) n", t=KT)
                                for n in range(SHIFT)]
                    else:
                        if not (isinstance(img, int) and img == 0):
                            sp.wait_ge(score_full, scores_before(img, True) + KT)
                        rows = [shift1[n:n + 1, :].rearrange("p (t n) -> p t n", t=KT) for n in range(SHIFT)]
                    for dst, src in zip(rows, neg):
                        sp.dma_start(dst.bitcast(F32), src[0:(HEADS if b == 0 else 1) * KT, :].bitcast(F32)).then_inc(shift_loaded[b], 16)
                elif name == "sums" and arg == 1:
                    sp.wait_ge(work_free, at + 1)
                    heads = HEADS if b == 0 else 1
                    for h in range(heads):
                        sp.dma_start(sums_dram[b][h:h + 1, :], rb[DH * h:DH * h + 1, :]).then_inc(sums_out[b], 16)
                    sp.wait_ge(sums_out[b], 16 * heads * (img + 1))
                    sp.dma_start(compact[b][:, :].rearrange("p (h e) -> p h e", h=heads),
                                 sums_dram[b].rearrange("h (p e) -> p h e", p=C)).then_inc(sums_in[b], 16)
                elif name == "recip":
                    heads = HEADS if b == 0 else 1
                    sp.wait_ge(recip_done[b], img + 1)
                    sp.dma_start(recip_dram[b].rearrange("h (p e) -> p h e", p=C),
                                 compact[b][:, :].rearrange("p (h e) -> p h e", h=heads)).then_inc(recip_out[b], 16)
                    sp.wait_ge(recip_out[b], 16 * (img + 1))
                    rows = C // heads
                    for h in range(heads):
                        sp.dma_start(rb[rows * h:rows * (h + 1), :],
                                     recip_dram[b][h:h + 1, :].to_broadcast([rows, N])).then_inc(rb_loaded[b], 16)
                elif name == "proj" and arg == 1:
                    sp.wait_ge(work_free, at + 1)
                    if b == 1:
                        sp.dma_start(out_dram[img], x1[:, par, :]).then_inc(stored, 16)
                    elif not (isinstance(img, int) and img + 2 >= images):
                        sp.dma_start(xin[:, par, :], x_dram[img + 2]).then_inc(x_loaded, 16)

            def run(steps, base, parity):
                n = base
                for s in steps:
                    step(s, parity_of(s, parity), n)
                    n = n + uses_work(s)

            run(background_start(), 0, 1)

            def body(i, parity):
                xs = background_x(i, images)
                run(xs, work_before_x(i), parity)
                run(background_y(i, images), work_before_y(i, xs), parity)

            bodies(sp, body)
            run(background_x(images, images), work_before_x(images), 0)
            run(background_x(images + 1, images), work_before_x(images + 1), 1)
            sp.wait_ge(stored, 16 * images)

        @block.gpsimd
        def _(pool):
            fills = [(ones[:, :].bitcast(F32), 1.0), (minus_half[:, :], -0.5), (shift1[:, :].bitcast(F32), 0.0)]
            fills += [(ks[p][SPLIT:C, :, :].bitcast(F32), 1.0) for p in range(2)]
            for n, (dst, value) in enumerate(fills):
                if n:
                    pool.wait_ge(pool_ready, n)
                pool.memset(dst, value).then_inc(pool_ready, 1)

            def rstd(b, img):
                pool.wait_ge(gn_chain[b], GN_CHAIN * img + 6)
                pool.tensor_tensor(gn[b][:, RSTD:RSTD + 1], gn[b][:, VAREPS:VAREPS + 1], minus_half[:, :],
                                   ALU.pow).then_inc(rstd_done[b], 1)

            def add(i, parity, y, kt, h):
                pool.wait_ge(probs_done, scores_before(i, y) + (kt if y else HEADS * kt + h) + 1)
                n = kt - 1 if y else HEADS * (kt - 1) + h
                total = sum1[:, :] if y else sum0[:, h, :]
                if kt == 1:
                    pool.wait_ge(pv_done, pv_before(i, y) + 1)
                else:
                    pool.wait_ge(pool_added, pool_adds_before(i, y) + (kt - 2 if y else POOL_HEADS * (kt - 2) + h) + 1)
                pool.tensor_tensor(total, total, probs[:, ring_slot(i, parity, y, n), :],
                                   ALU.add).then_inc(pool_added, 1)

            pool.wait_ge(pool_ready, 5)
            rstd(0, 0)

            RSTD_AT = 3

            def body(i, parity):
                if not (isinstance(i, int) and i + 1 >= images):
                    rstd(0, i + 1)
                for kt in range(1, KT):
                    for h in range(POOL_HEADS):
                        add(i, parity, False, kt, h)
                if not (isinstance(i, int) and i == 0):
                    for kt in range(1, KT):
                        add(i, parity, True, kt, 0)
                        if kt == RSTD_AT:
                            rstd(1, i)
                else:
                    rstd(1, i)

            bodies(pool, body)
            for kt in range(1, KT):
                add(images, 0, True, kt, 0)

        @block.scalar
        def _(act):
            def exp(i, parity, y, kt, h):
                n = kt if y else HEADS * kt + h
                act.wait_ge(score_full, scores_before(i, y) + n + 1)
                if kt == 0:
                    dst = sum1[:, :] if y else sum0[:, h, :]
                    if y and not (isinstance(i, int) and i == 1):
                        act.wait_ge(work_full, x_position(i, "sums1", 1) + 1)
                    if y:
                        act.wait_ge(stacked, 16 * STACK_DMAS * (images if isinstance(i, int) and i + 2 > images else i + 2))
                    if not y and h == 0 and not (isinstance(i, int) and i == 0):
                        act.wait_ge(work_full, y_position(i - 1, "sums0", 1) + 1)
                else:
                    r = n - 1 if y else n - HEADS
                    free_probs(i, y, r)
                    dst = probs[:, ring_slot(i, parity, y, r), :]
                act.activation(dst, score[n % 2][:, :], ACT.Exp, scale=SCALE).then_inc(probs_done, 1)

            def free_probs(i, y, r):
                u = r - P_RING
                per_x = (KT - 1) * HEADS
                if y and u < 0 and not (isinstance(i, int) and i >= images):
                    y, u = False, u + per_x
                elif u < 0:
                    if isinstance(i, int) and i <= 1:
                        if i == 0:
                            return
                        i, y, u = 0, False, u + per_x
                    else:
                        i, y, u = i - 1, True, u + KT - 1
                        if u < 0:
                            y, u = False, u + per_x
                if y:
                    act.wait_ge(pv_done, pv_before(i, True) + u + 2)
                    act.wait_ge(pool_added, pool_adds_before(i, True) + u + 1)
                    return
                kt, h = u // HEADS + 1, u % HEADS
                act.wait_ge(pv_done, pv_before(i, False) + kt + 1)
                if h < POOL_HEADS:
                    act.wait_ge(pool_added, pool_adds_before(i, False) + POOL_HEADS * (kt - 1) + h + 1)
                else:
                    act.wait_ge(dve_added, (KT - 1) * i + kt)

            def save(i, y):
                act.wait_ge(pv_done, pv_before(i, y) + KT)
                if y:
                    if not (isinstance(i, int) and i >= images):
                        act.wait_ge(work_full, y_position(i, "proj0", 1) + 1)
                    else:
                        act.wait_ge(work_full, x_position(i, "proj1", 1) + 1)
                elif not (isinstance(i, int) and i < 2):
                    act.wait_ge(work_full, x_position(i, "proj1", 1) + 1)
                act.copy(mix[:, :], acc[:, :]).then_inc(saved, 1)

            def body(i, parity):
                for kt in range(KT):
                    for h in range(HEADS):
                        exp(i, parity, False, kt, h)
                    if kt == 0 and not (isinstance(i, int) and i < 2):
                        save(i - 1, True)
                if isinstance(i, int) and i == 0:
                    save(0, False)
                    return
                for kt in range(KT):
                    exp(i, parity, True, kt, 0)
                    if kt == 0:
                        save(i, False)

            bodies(act, body)
            save(images - 1, True)
            for kt in range(KT):
                exp(images, 0, True, kt, 0)
            save(images, True)

        @block.vector
        def _(dve):
            def step(s, par, at, bank):
                name, img, arg = s
                b = int(name[-1])
                name = name[:-1]
                chain = gn_chain[b]
                g = gn[b]
                first = isinstance(img, int) and img == 0

                def col(n):
                    return g[:, n:n + 1]

                def full():
                    dve.wait_ge(work_full, at + 1)

                if name == "stats":
                    src = xin[:, par, :] if b == 0 else x1[:, par, :]
                    if b == 0:
                        dve.wait_ge(x_loaded, 16 * (img + 1))
                    else:
                        dve.wait_ge(x1_done, 2 * (img + 1))
                    for h in range(2):
                        dve.bn_stats(stats[b][:, h, :], src[:, halves(h)]).then_inc(chain, 1)
                    dve.wait_ge(chain, GN_CHAIN * img + 2)
                    dve.tensor_copy(col(GAIN), stats[b][:, 0, 0:1])
                    dve.bn_aggr(mv[b][:, :], stats[b][:, :, :]).then_inc(chain, 1)
                elif name == "mean":
                    full()
                    dve.tensor_tensor(col(DIFF), mv[b][:, 0:1], work[bank][:, 0:1], ALU.subtract).then_inc(chain, 1)
                    dve.tensor_copy(col(GMEAN), work[bank][:, 0:1]).then_inc(work_free, 1)
                    dve.wait_ge(chain, GN_CHAIN * img + 4)
                    dve.scalar_tensor_tensor(out=col(VARIN), in0=col(DIFF), scalar=col(DIFF), in1=mv[b][:, 1:2],
                                             op0=ALU.mult, op1=ALU.add).then_inc(chain, 1)
                elif name == "var":
                    full()
                    dve.tensor_scalar(col(VAREPS), work[bank][:, 0:1], EPS[b], None, ALU.add).then_inc(chain, 1)
                    dve.wait_ge(chain, GN_CHAIN * img + 6)
                    dve.tensor_copy(col(MG), work[bank][:, 0:1]).then_inc(work_free, 1)
                elif name == "norm":
                    dve.wait_ge(rstd_done[b], img + 1)
                    dve.tensor_tensor(col(GAIN), col(RSTD), vec(b, GAMMA), ALU.mult).then_inc(chain, 1)
                    dve.wait_ge(chain, GN_CHAIN * img + 7)
                    dve.tensor_tensor(col(MG), col(GMEAN), col(GAIN), ALU.mult).then_inc(chain, 1)
                    dve.wait_ge(chain, GN_CHAIN * img + 8)
                    dve.tensor_tensor(col(OFFSET), vec(b, BETA), col(MG), ALU.subtract).then_inc(chain, 1)
                    dve.wait_ge(chain, GN_CHAIN * img + 9)
                    src = xin[:, par, :] if b == 0 else x1[:, par, :]
                    dve.tensor_scalar(xh[:, :], src, col(GAIN), col(OFFSET), ALU.mult, ALU.add).then_inc(chain, 1)
                elif name in ("q", "k"):
                    full()
                    which = 0 if name == "q" else 1
                    if b == 0:
                        hi, lo = part[2 * which], part[2 * which + 1]
                        if arg == 0 and not first:
                            dve.wait_ge(stacked, 16 * STACK_DMAS * img)
                        if name == "q" and arg == 0 and not (isinstance(img, int) and img < 2):
                            dve.wait_ge(score_full, scores_before(img - 2, False) + KT * HEADS)
                    else:
                        hi, lo = part1[2 * which], part1[2 * which + 1]
                        if name == "q" and arg == 0 and not first:
                            dve.wait_ge(score_full, scores_before(img, True) + KT)
                    bias = vec(b, BQ if which == 0 else BK)
                    dve.tensor_scalar(hi[:, halves(arg)], work[bank][:, :], bias, None, ALU.add).then_inc(hi_done[b], 1)
                    dve.wait_ge(hi_done[b], 4 * img + 2 * which + arg + 1)
                    dve.scalar_tensor_tensor(out=lo[:, halves(arg)], in0=work[bank][:, :], scalar=bias,
                                             in1=hi[:, halves(arg)].bitcast(F32), op0=ALU.add,
                                             op1=ALU.subtract).then_inc(work_free, 1)
                elif name == "v":
                    full()
                    if b == 0 and arg == 0 and not (isinstance(img, int) and img < 2):
                        dve.wait_ge(pv_done, pv_before(img - 2, False) + KT)
                    if b == 1 and arg == 0 and not first:
                        dve.wait_ge(pv_done, pv_before(img, True) + KT)
                    dst = v0[:, par, :, :] if b == 0 else v1[:, :, :]
                    dve.tensor_copy(dst[:, 4 * arg:4 * arg + 4, :].rearrange("p t n -> p (t n)"),
                                    work[bank][:, :]).then_inc(work_free, 1)
                elif name == "max":
                    full()
                    dve.tensor_reduce(halfmax[b][:, arg // 2, arg % 2:arg % 2 + 1], work[bank][:, :], AX.X,
                                      ALU.max).then_inc(work_free, 1)
                elif name == "gather":
                    dve.wait_ge(work_free, at)
                    dve.tensor_reduce(rowmax[b][:, :], halfmax[b][:, :, :], AX.X, ALU.max).then_inc(rowmax_done[b], 1)
                elif name == "shift":
                    full()
                    rows = (HEADS if b == 0 else 1) * KT
                    src = work[bank][0:rows, 0:C]
                    neg_hi, neg_lo = (n[0:rows, :] for n in neg)
                    if b == 1:
                        dve.wait_ge(shift_loaded[0], 32 * (images if isinstance(img, int) and img + 2 > images else img + 2))
                    elif not (isinstance(img, int) and img < 2):
                        dve.wait_ge(shift_loaded[1], 32 * (img - 1))
                    elif not first:
                        dve.wait_ge(shift_loaded[0], 32 * img)
                    dve.tensor_scalar(neg_hi, src, -1.0, None, ALU.mult).then_inc(neg_done[b], 1)
                    dve.wait_ge(neg_done[b], img + 1)
                    dve.scalar_tensor_tensor(out=neg_lo, in0=src, scalar=-1.0, in1=neg_hi.bitcast(F32),
                                             op0=ALU.mult, op1=ALU.subtract).then_inc(work_free, 1)
                elif name == "sums":
                    full()
                    dve.tensor_copy(rb[:, halves(arg)], work[bank][:, :]).then_inc(work_free, 1)
                elif name == "recip":
                    dve.wait_ge(sums_in[b], 16 * (img + 1))
                    dve.reciprocal(compact[b][:, :], compact[b][:, :]).then_inc(recip_done[b], 1)
                elif name == "scale":
                    dve.wait_ge(rb_loaded[b], 16 * (HEADS if b == 0 else 1) * (img + 1))
                    dve.wait_ge(saved, saved_before(img, False) + 1 if b == 0 else saved_before(img + 1, True) + 1)
                    dve.tensor_tensor(mix[:, :], mix[:, :], rb[:, :], ALU.mult).then_inc(scaled[b], 1)
                elif name == "proj":
                    full()
                    dst = x1[:, par, halves(arg)]
                    if b == 0 and arg == 0 and not (isinstance(img, int) and img < 2):
                        dve.wait_ge(stored, 16 * (img - 1))
                    res = xin[:, par, halves(arg)] if b == 0 else dst
                    dve.scalar_tensor_tensor(out=dst, in0=work[bank][:, :], scalar=proj_bias[:, b:b + 1], in1=res,
                                             op0=ALU.add, op1=ALU.add).then_inc(work_free, 1)
                    if b == 0:
                        dve.wait_ge(work_free, at + 1)
                        dve.tensor_scalar(dst, dst, math.sqrt(0.5), None, ALU.mult).then_inc(x1_done, 1)

            def add(i, parity, kt):
                h = HEADS - 1
                dve.wait_ge(probs_done, scores_before(i, False) + HEADS * kt + h + 1)
                if kt == 1:
                    dve.wait_ge(pv_done, pv_before(i, False) + 1)
                else:
                    dve.wait_ge(dve_added, (KT - 1) * i + kt - 1)
                dve.tensor_tensor(sum0[:, h, :], sum0[:, h, :], probs[:, ring_slot(i, parity, False, HEADS * (kt - 1) + h), :],
                                  ALU.add).then_inc(dve_added, 1)

            dve.wait_ge(const_loaded, 48)
            for b in range(2):
                dve.wait_ge(bias_ready, b + 1)
                dve.tensor_tensor(proj_bias[:, b:b + 1], acc[:, HALF * b:HALF * b + 1], vec(b, BP),
                                  ALU.add).then_inc(dve_setup, 1)
            dve.wait_ge(dve_setup, 2)

            def run(steps, at, bank, parity):
                for s in steps:
                    step(s, parity_of(s, parity), at, bank)
                    if uses_work(s):
                        at, bank = at + 1, 1 - bank
                return at, bank

            run(background_start(), 0, 0, 1)

            def body(i, parity):
                at, bank = work_before_x(i), work_parity(i, parity, False)
                for g, steps in enumerate(gaps_x(i)):
                    at, bank = run(steps, at, bank, parity)
                    if g % HEADS == HEADS - 1 and g // HEADS >= 2:
                        add(i, parity, g // HEADS - 1)
                for g, steps in enumerate(gaps_y(i)):
                    at, bank = run(steps, at, bank, parity)
                    if g == 0:
                        add(i, parity, KT - 1)

            bodies(dve, body)
            run(background_x(images, images), work_before_x(images), work_parity(images, 0, False), 0)
            run(background_x(images + 1, images), work_before_x(images + 1), work_parity(images + 1, 1, False), 1)

        @block.tensor
        def _(pe):
            def step(s, par, at, bank):
                name, img, arg = s
                b = int(name[-1])
                name = name[:-1]
                out_bank = work[bank]
                if not uses_work(s):
                    return
                if not (isinstance(at, int) and at < 2):
                    pe.wait_ge(work_free, at - 1)
                if name == "mean":
                    pe.wait_ge(gn_chain[b], GN_CHAIN * img + 3)
                    mm = pe.matmul(out_bank[:, 0:1], consts[:, 1 + b, :], mv[b][:, 0:1], start=True, stop=True)
                elif name == "var":
                    pe.wait_ge(gn_chain[b], GN_CHAIN * img + 5)
                    mm = pe.matmul(out_bank[:, 0:1], consts[:, 1 + b, :], gn[b][:, VARIN:VARIN + 1], start=True, stop=True)
                elif name in ("q", "k"):
                    pe.wait_ge(gn_chain[b], GN_CHAIN * img + 10)
                    mm = pe.matmul(out_bank[:, :], w(b, WQ if name == "q" else WK), xh[:, halves(arg)], start=True, stop=True)
                elif name == "v":
                    for t in range(4):
                        mm = pe.matmul(out_bank[:, tile(t)], xh[:, tile(4 * arg + t)], w(b, WV), start=True, stop=True)
                elif name == "max":
                    t, half = arg // 2, arg % 2
                    if b == 0:
                        h, t = t // KT, t % KT
                        if arg == 0:
                            pe.wait_ge(stacked, 16 * STACK_DMAS * (img + 1))
                        mm = pe.matmul(out_bank[:, :], qs[par][0:SPLIT, h, tile(t)], ks[par][0:SPLIT, h, halves(half)],
                                       start=True, stop=True)
                    else:
                        if arg == 0:
                            pe.wait_ge(hi_done[1], 4 * (img + 1))
                        mm = pe.matmul(out_bank[:, :], part1[0][:, tile(t)], part1[2][:, halves(half)], start=True, stop=True)
                elif name == "shift":
                    pe.wait_ge(rowmax_done[b], img + 1)
                    rows = (HEADS if b == 0 else 1) * KT
                    mm = pe.transpose(out_bank[0:rows, 0:C], rowmax[b][:, :], identity)
                elif name == "sums":
                    if b == 0:
                        pe.wait_ge(pool_added, pool_adds_before(img, False) + (KT - 1) * POOL_HEADS)
                        pe.wait_ge(dve_added, (KT - 1) * (img + 1))
                        for h in range(HEADS):
                            mm = pe.matmul(out_bank[head(h), :], ones[:, 0:DH].bitcast(F32), sum0[:, h, halves(arg)], start=True,
                                           stop=True, tile_position=(0, DH * h))
                    else:
                        pe.wait_ge(pool_added, pool_adds_before(img + 1, True) + KT - 1)
                        mm = pe.matmul(out_bank[:, :], ones[:, :].bitcast(F32), sum1[:, halves(arg)], start=True, stop=True)
                elif name == "proj":
                    pe.wait_ge(scaled[b], img + 1)
                    mm = pe.matmul(out_bank[:, :], w(b, WP), mix[:, halves(arg)], start=True, stop=True)
                mm.then_inc(work_full, 1)

            def scores0(i, parity, kt, h):
                n = HEADS * kt + h
                if kt == 0 and h == 0:
                    pe.wait_ge(shift_loaded[0], 32 * (i + 1))
                if not (isinstance(i, int) and i == 0 and n < 2):
                    pe.wait_ge(probs_done, scores_before(i, False) + n - 1)
                for half in range(2):
                    mm = pe.matmul(score[n % 2][:, halves(half)], ks[parity][0:SPLIT + SHIFT, h, tile(kt)],
                                   qs[parity][0:SPLIT + SHIFT, h, halves(half)], start=True, stop=True)
                mm.then_inc(score_full, 1)

            def scores1(i, kt):
                if kt == 0:
                    pe.wait_ge(shift_loaded[1], 32 * i)
                pe.wait_ge(probs_done, scores_before(i, True) + kt - 1)
                q_hi, q_lo, k_hi, k_lo = part1
                for half in range(2):
                    dst = score[kt % 2][:, halves(half)]
                    pe.matmul(dst, k_hi[:, tile(kt)], q_hi[:, halves(half)], start=True, stop=False)
                    pe.matmul(dst, k_hi[:, tile(kt)], q_lo[:, halves(half)], start=False, stop=False)
                    pe.matmul(dst, k_lo[:, tile(kt)], q_hi[:, halves(half)], start=False, stop=False)
                    mm = pe.matmul(dst, ones[:, :], shift1[:, halves(half)], start=False, stop=True)
                mm.then_inc(score_full, 1)

            def pv(i, parity, y, kt, half):
                if half == 0:
                    pe.wait_ge(probs_done, scores_before(i, y) + (kt + 1 if y else HEADS * (kt + 1)))
                    if kt == 0 and not (isinstance(i, int) and i == 0):
                        pe.wait_ge(saved, saved_before(i, y))
                for h in range(1 if y else HEADS):
                    if y:
                        dst, v = acc[:, halves(half)], v1[:, kt, :]
                        src = sum1[:, halves(half)] if kt == 0 else probs[:, ring_slot(i, parity, True, kt - 1), halves(half)]
                        where = None
                    else:
                        dst, v = acc[head(h), halves(half)], v0[:, parity, kt, head(h)]
                        src = sum0[:, h, halves(half)] if kt == 0 else \
                            probs[:, ring_slot(i, parity, False, HEADS * (kt - 1) + h), halves(half)]
                        where = (0, DH * h)
                    mm = pe.matmul(dst, v, src, start=kt == 0, stop=kt == KT - 1, tile_position=where)
                if half == 1:
                    mm.then_inc(pv_done, 1)

            pe.wait_ge(const_loaded, 48)
            for b in range(2):
                pe.matmul(acc[:, HALF * b:HALF * b + 1], w(b, WP), vec(b, BV), start=True, stop=True).then_inc(bias_ready, 1)
            pe.wait_ge(dve_setup, 2)
            pe.wait_ge(pool_ready, 5)

            def run(steps, at, bank, parity):
                for s in steps:
                    step(s, parity_of(s, parity), at, bank)
                    if uses_work(s):
                        at, bank = at + 1, 1 - bank
                return at, bank

            run(background_start(), 0, 0, 1)

            def body(i, parity):
                at, bank = work_before_x(i), work_parity(i, parity, False)
                gaps = gaps_x(i)
                for kt in range(KT):
                    if kt > 0:
                        before = (i, parity, False, kt - 1)
                    elif isinstance(i, int) and i < 2:
                        before = (0, 0, False, KT - 1) if i == 1 else None
                    else:
                        before = (i - 1, 1 - parity, True, KT - 1)
                    if isinstance(i, int) and i == 1 and kt == 0:
                        before = None
                    for h in range(HEADS):
                        scores0(i, parity, kt, h)
                        at, bank = run(gaps[HEADS * kt + h], at, bank, parity)
                        if h % 2 and before:
                            pv(*before, h // 2)
                gaps = gaps_y(i)
                if isinstance(i, int) and i == 0:
                    for half in range(2):
                        pv(i, parity, False, KT - 1, half)
                    for steps in gaps:
                        at, bank = run(steps, at, bank, parity)
                    return
                for kt in range(KT):
                    scores1(i, kt)
                    before = (i, parity, True, kt - 1) if kt else (i, parity, False, KT - 1)
                    for half in range(2):
                        at, bank = run(gaps[2 * kt + half], at, bank, parity)
                        pv(*before, half)

            bodies(pe, body)
            for half in range(2):
                pv(images - 1, 1, True, KT - 1, half)
            run(background_x(images, images), work_before_x(images), work_parity(images, 0, False), 0)
            for kt in range(KT):
                scores1(images, kt)
                if kt:
                    for half in range(2):
                        pv(images, 0, True, kt - 1, half)
            for half in range(2):
                pv(images, 0, True, KT - 1, half)
            run(background_x(images + 1, images), work_before_x(images + 1), work_parity(images + 1, 1, False), 1)


def kernel(**inputs):
    import numpy as np
    import concourse.bacc as bacc
    from concourse.bass_utils import run_bass_kernel_spmd as run

    a = {k: np.ascontiguousarray(v) for k, v in inputs.items()}
    wq1, wk1, wv1 = a["L1_conv_qkv_w"].reshape(3, C, C)
    weights = np.ascontiguousarray(np.stack(
        [a["L0_conv_Wq"], a["L0_conv_Wk"], a["L0_conv_Wv"], a["L0_conv_Wp"],
         wq1.T, wk1.T, wv1.T, a["L1_conv_proj_w"].T], axis=1))
    bq1, bk1, bv1 = a["L1_conv_qkv_b"].reshape(3, C)
    vectors = np.ascontiguousarray(np.stack(
        [a["L0_conv_gn_scale"], a["L0_conv_gn_bias"], a["L0_conv_bq"], a["L0_conv_bk"], a["L0_conv_bv"],
         a["L0_conv_bp"], a["L1_conv_gn_w"], a["L1_conv_gn_b"], bq1, bk1, bv1, a["L1_conv_proj_b"]], axis=1))
    channel = np.arange(C)
    constants = np.stack(
        [np.eye(C)] + [(channel[:, None] // g == channel[None, :] // g) / g for g in (C // 32, C // 8)],
        axis=1).astype(np.float32)
    arrays = {"x_dram": a["x"], "weights_dram": weights, "vectors_dram": vectors,
              "constants_dram": np.ascontiguousarray(constants)}

    nc = bacc.Bacc("TRN2", target_bir_lowering=False, num_devices=1)
    args = [nc.dram_tensor(n, v.shape, mybir.dt.from_np(v.dtype), kind="ExternalInput").ap() for n, v in arrays.items()]
    out = nc.dram_tensor("out_0_dram", a["x"].shape, F32, kind="ExternalOutput").ap()
    bass_two_attention_blocks(nc, *args, out)
    return run(nc, [arrays], core_ids=[0]).results[0]["out_0_dram"]
```

```python
from contextlib import ExitStack
import math

import concourse.bass as bass
from concourse import mybir

F32 = mybir.dt.float32
F32R = mybir.dt.float32r
ALU = mybir.AluOpType
ACT = mybir.ActivationFunctionType
AX = mybir.AxisListType

C = 128
N = 1024
HALF = 512
KT = N // C
HEADS = 4
DH = C // HEADS
SPLIT = 3 * DH
SHIFT = 2
NVEC = 12
P_RING = 10
SCALE = 1.0 / math.sqrt(C)
EPS = (1e-6, 1e-5)

BANKS = 4
WQ, WK, WV, WP = range(4)
GAMMA, BETA, BQ, BK, BV, BP = range(6)
MAXES_IN_X = 24

X_GAPS, Y_GAPS = 6, 4

BESIDE_X = [("sums1", -2, 1), ("q1", -1, 0), ("k1", -1, 5), ("v1", -1, 8), ("q0", 1, 13), ("k0", 1, 15),
            ("v0", 1, 19)]
BESIDE_Y = [("sums0", 0, 1)]


def gap_x(name):
    n = [n for step, _, n in BESIDE_X if step == name][0]
    kt, h = divmod(n, HEADS)
    return X_GAPS * kt + h + h // 2 + 1 - h % 2


PLACE_X = [("stats0", 1, 0, 0), ("mean0", 1, 0, 2), ("splitq1", -1, 0, gap_x("q1") + 1),
           ("splitk1", -1, 0, gap_x("k1") + 2), ("var0", 1, 0, 6), ("norm0", 1, 0, 16), ("recip1", -2, 0, 12),
           ("splitq0", 1, 0, gap_x("q0") + 1), ("splitk0", 1, 0, gap_x("k0") + 2), ("scale1", -2, 0, 27),
           ("proj1", -2, 0, 31), ("proj1", -2, 1, 0), ("gather1", -1, 0, 32), ("shift1", -1, 0, 36)]
PLACE_Y = [("add0", 0, 0, 1), ("recip0", 0, 0, 11), ("scale0", 0, 0, 17), ("proj0", 0, 0, 18),
           ("proj0", 0, 1, 0), ("stats1", 0, 0, 18), ("mean1", 0, 0, 23), ("var1", 0, 0, 22), ("norm1", 0, 0, 25),
           ("gather0", 1, 0, 25), ("shift0", 1, 0, 27)]
MAXIMA_X = [("max1", -1, range(2 * KT), gap_x("k1") + 12, 33),
            ("max0", 1, range(MAXES_IN_X), gap_x("k0") + 14, X_GAPS * KT)]
MAXIMA_Y = [("max0", 1, range(MAXES_IN_X, 2 * KT * HEADS), 0, 26)]

WEIGHT = {"stats": 2, "mean": 1, "var": 1, "max": 1, "norm": 1, "splitq": 2, "splitk": 2, "recip": 0,
          "scale": 2, "gather": 0, "shift": 1, "proj": 1, "add": 3}


def present(image, images):
    return not isinstance(image, int) or 0 <= image < images


def spread(places, maxima, gaps, i, images):
    fixed, at = [[] for _ in range(gaps)], 0
    for name, ahead, arg, gap in places:
        at = max(at, gap)
        if present(i + ahead, images):
            fixed[at].append((name, i + ahead, arg))
    out = [[] for _ in range(gaps)]

    def weight(steps):
        return sum(WEIGHT[s[0][:-1]] for s in steps)

    for name, ahead, numbers, first, end in maxima:
        if not present(i + ahead, images):
            continue
        rate = 0.0
        while True:
            left, placed, total = list(numbers), [[] for _ in range(gaps)], 0.0
            for g in range(first, end):
                total += weight(fixed[g]) + weight(out[g])
                while left and total < rate * (g - first + 1):
                    placed[g].append((name, i + ahead, left.pop(0)))
                    total += 1
            if not left:
                break
            rate += 0.02
        out = [a + b for a, b in zip(out, placed)]
    return [m + f for m, f in zip(out, fixed)]


def gaps_x(i, images):
    return spread(PLACE_X, MAXIMA_X, X_GAPS * KT, i, images)


def gaps_y(i, images):
    return spread(PLACE_Y, MAXIMA_Y, Y_GAPS * KT, i, images)


def work_steps_x(i, images):
    return sum(gaps_x(i, images), [])


def work_steps_y(i, images):
    return sum(gaps_y(i, images), [])


def score_steps_x(i, images):
    steps = []
    for n in range(KT * HEADS):
        if present(i, images):
            steps.append(("exp0", i, divmod(n, HEADS)))
        steps += [(name, i + ahead, None) for name, ahead, at in BESIDE_X if at == n and present(i + ahead, images)]
    return steps


def score_steps_y(i, images):
    steps = []
    for kt in range(KT):
        if present(i - 1, images):
            steps.append(("exp1", i - 1, (kt, 0)))
        steps += [(name, i + ahead, None) for name, ahead, at in BESIDE_Y if at == kt and present(i + ahead, images)]
    return steps


START = ([("stats0", 0, 0), ("mean0", 0, 0), ("var0", 0, 0), ("norm0", 0, 0), ("q0", 0, None),
          ("splitq0", 0, 0), ("k0", 0, None), ("splitk0", 0, 0), ("v0", 0, None)]
         + [("max0", 0, n) for n in range(2 * KT * HEADS)] + [("gather0", 0, 0), ("shift0", 0, 0)])

WORK = ("mean", "var", "max", "shift", "proj")
SCORE = ("exp", "sums", "q", "k", "v")


def uses_work(step):
    return step[0][:-1] in WORK


def work_count(steps):
    return sum(map(uses_work, steps))


def score_count(steps):
    return 2 * sum(s[0][:-1] in SCORE for s in steps)


def bass_two_attention_blocks(nc, x, weights, vectors, constants, out):
    images = x.shape[0]
    x_dram = x.rearrange("b c h w -> b c (h w)")
    out_dram = out.rearrange("b c h w -> b c (h w)")

    def counter(count, steps_x, steps_y, start):
        per_body = count(steps_x(5, images)) + count(steps_y(5, images))

        def before_x(i):
            if isinstance(i, int) and (i < 2 or i >= images):
                at, first = (start, 0) if i < 2 else (before_x(images - 1), images - 1)
                for n in range(first, i):
                    at += count(steps_x(n, images)) + count(steps_y(n, images))
                return at
            return before_x(1) + count(steps_x(1, images)) + count(steps_y(1, images)) + (i - 2) * per_body

        def before(i, y):
            return before_x(i) + (count(steps_x(i, images)) if y else 0)

        return before, per_body

    work_before, work_per_body = counter(work_count, work_steps_x, work_steps_y, work_count(START))
    scores_before, _ = counter(score_count, score_steps_x, score_steps_y, score_count(START))

    def score_position(i, y, name, arg=None):
        n = 0
        for s in (score_steps_y if y else score_steps_x)(i, images):
            if (s[0], s[2]) == (name, arg):
                return scores_before(i, y) + 2 * n
            n += 1
        raise KeyError((name, arg))

    def exp_position(i, y, kt, h=0):
        return score_position(i, y, "exp1" if y else "exp0", (kt, h))

    def before_x(i, x_count, y_count):
        return 0 if isinstance(i, int) and i == 0 else (x_count + y_count) * i - y_count

    def before_y(i, x_count, y_count):
        if isinstance(i, int) and i >= images:
            return before_x(i, x_count, y_count)
        return before_x(i, x_count, y_count) + x_count

    def ring_before(i, y):
        return (before_y if y else before_x)(i, (KT - 1) * HEADS, KT - 1)

    def pv_before(i, y):
        return (before_y if y else before_x)(i, KT, KT)

    POOL_HEADS = 3
    DVE_HEADS = HEADS - POOL_HEADS

    def pool_adds_before(i, y):
        return (before_y if y else before_x)(i, (KT - 1) * POOL_HEADS, KT - 1)

    def saved_before(i, y):
        return (before_y if y else before_x)(i, 1, 1)

    def ring_slot(i, parity, y, n):
        j = i if isinstance(i, int) else 2 + parity
        return (ring_before(j, y) + n) % P_RING

    with ExitStack() as ctx:
        def sb(name, shape, dt=F32):
            return ctx.enter_context(nc.sbuf_tensor(name, shape, dt))

        def ps(name, shape, dt=F32):
            return ctx.enter_context(nc.psum_tensor(name, shape, dt))

        def sem(name):
            return ctx.enter_context(nc.semaphore(name))

        wts = sb("wts", [C, 8, C])
        vecs = sb("vecs", [C, NVEC])
        consts = sb("consts", [C, 3, C])
        ones = sb("ones", [C, C], F32R)
        minus_half = sb("minus_half", [C, 1])
        xin = sb("xin", [C, 2, N])
        x1 = sb("x1", [C, 2, N])
        xh = sb("xh", [C, N])
        part = [sb(n, [C, N], F32R) for n in ("q_hi", "q_lo", "k_hi", "k_lo")]
        qs = [sb(f"q_stack{p}", [C, HEADS, N], F32R) for p in range(2)]
        ks = [sb(f"k_stack{p}", [C, HEADS, N], F32R) for p in range(2)]
        part1 = [sb(n, [C, N], F32R) for n in ("q1_hi", "q1_lo", "k1_hi", "k1_lo")]
        shift1 = sb("shift1", [C, N], F32R)
        v0 = sb("v0", [C, 2, KT, C])
        v1 = sb("v1", [C, KT, C])
        probs = sb("probs", [C, P_RING, N])
        sum0 = sb("sum0", [C, HEADS, N])
        sum1 = part[0][:, :].bitcast(F32)
        mix = sb("mix", [C, N])
        rb = sb("rb", [C, N])
        compact = [sb(f"compact{b}", [C, h * KT]) for b, h in ((0, HEADS), (1, 1))]
        halfmax = [sb(f"halfmax{b}", [C, h * KT, 2]) for b, h in ((0, HEADS), (1, 1))]
        rowmax = [sb(f"rowmax{b}", [C, h * KT]) for b, h in ((0, HEADS), (1, 1))]
        neg = [sb(n, [HEADS * KT, C], F32R) for n in ("neg_hi", "neg_lo")]
        stats = [sb(f"stats{b}", [C, 2, 6]) for b in range(2)]
        mv = [sb(f"mv{b}", [C, 2]) for b in range(2)]
        gn = [sb(f"gn{b}", [C, 8]) for b in range(2)]
        proj_bias = sb("proj_bias", [C, 2])
        DIFF, GMEAN, VARIN, VAREPS, RSTD, GAIN, MG, OFFSET = range(8)

        sums_dram = [nc.dram_tensor(f"sums_dram{b}", (h, N), F32).ap() for b, h in ((0, HEADS), (1, 1))]
        recip_dram = [nc.dram_tensor(f"recip_dram{b}", (h, N), F32).ap() for b, h in ((0, HEADS), (1, 1))]

        score = [ps(f"score{n}", [C, HALF]) for n in range(2)]
        acc = ps("acc", [C, N])
        work = [ps(f"work{n}", [C, HALF]) for n in range(BANKS)]

        const_loaded = sem("const_loaded")
        pool_ready = sem("pool_ready")
        bias_ready = sem("bias_ready")
        x_loaded = sem("x_loaded")
        work_full = sem("work_full")
        work_free = sem("work_free")
        split_done = [sem(f"split_done{b}") for b in range(2)]
        neg_done = [sem(f"neg_done{b}") for b in range(2)]
        bias_added = sem("bias_added")
        gn_chain = [sem(f"gn_chain{b}") for b in range(2)]
        GN_CHAIN = 10
        rstd_done = [sem(f"rstd_done{b}") for b in range(2)]
        stacked = sem("stacked")
        STACK_DMAS = 6 * HEADS
        rowmax_done = [sem(f"rowmax_done{b}") for b in range(2)]
        shift_loaded = [sem(f"shift_loaded{b}") for b in range(2)]
        act_full = sem("act_full")
        act_done = sem("act_done")
        pv_done = sem("pv_done")
        pool_added = sem("pool_added")
        dve_added = sem("dve_added")
        saved = sem("saved")
        sums_out = [sem(f"sums_out{b}") for b in range(2)]
        sums_in = [sem(f"sums_in{b}") for b in range(2)]
        recip_done = [sem(f"recip_done{b}") for b in range(2)]
        recip_out = [sem(f"recip_out{b}") for b in range(2)]
        rb_loaded = [sem(f"rb_loaded{b}") for b in range(2)]
        scaled = [sem(f"scaled{b}") for b in range(2)]
        x1_done = sem("x1_done")
        stored = sem("stored")

        def w(b, which):
            return wts[:, 4 * b + which, :]

        def vec(b, which):
            return vecs[:, 6 * b + which:6 * b + which + 1]

        identity = consts[:, 0, :]

        def heads_of(b):
            return HEADS if b == 0 else 1

        def halves(h):
            return slice(HALF * h, HALF * (h + 1))

        def tile(t):
            return slice(C * t, C * (t + 1))

        def head(h):
            return slice(DH * h, DH * (h + 1))

        def work_position(i, y, name, arg=0):
            n = 0
            for s in (work_steps_y if y else work_steps_x)(i, images):
                if (s[0], s[2]) == (name, arg):
                    return work_before(i, y) + n
                n += uses_work(s)
            raise KeyError((name, arg))

        assert 2 * work_per_body % BANKS == 0, "an iteration of the loop has to leave the banks as it found them"

        def first_bank(i, parity):
            return work_before(i if isinstance(i, int) else 2 + parity, False) % BANKS

        def parity_of(s, parity):
            name, b = s[0][:-1], int(s[0][-1])
            same = name in ("sums", "recip", "scale", "proj", "add") or (b == 1 and name in ("stats", "mean", "var", "norm"))
            return parity if same else 1 - parity

        def bodies(engine, body):
            body(0, 0)
            body(1, 1)
            with engine.Fori(1, images // 2 - 1) as pair:
                body(2 * pair, 0)
                body(2 * pair + 1, 1)
            body(images - 2, 0)
            body(images - 1, 1)

        block = ctx.enter_context(nc.Block())

        @block.sync
        def _(sp):
            sp.dma_start(xin[:, 0, :], x_dram[0]).then_inc(x_loaded, 16)
            sp.dma_start(wts[:, :, :], weights).then_inc(const_loaded, 16)
            sp.dma_start(vecs[:, :], vectors).then_inc(const_loaded, 16)
            sp.dma_start(consts[:, :, :], constants).then_inc(const_loaded, 16)
            sp.dma_start(xin[:, 1, :], x_dram[1]).then_inc(x_loaded, 16)

            def stack(img, par, which):
                hi, lo = part[2 * which], part[2 * which + 1]
                dst = (qs, ks)[which][par]
                sp.wait_ge(split_done[0], 2 * img + which + 1)
                for group, src in enumerate((hi, lo, hi) if which == 0 else (hi, hi, lo)):
                    for h in range(HEADS):
                        sp.dma_start(dst[DH * group:DH * (group + 1), h, :].bitcast(F32),
                                     src[head(h), :].bitcast(F32)).then_inc(stacked, 16)

            def load_shift(b, img, par, at):
                if b == 0:
                    rows = [qs[par][SPLIT + n:SPLIT + n + 1, :, :].rearrange("p h (t n) -> p (h t) n", t=KT)
                            for n in range(SHIFT)]
                else:
                    rows = [shift1[n:n + 1, :].rearrange("p (t n) -> p t n", t=KT) for n in range(SHIFT)]
                sp.wait_ge(work_free, at + 1)
                for dst, src in zip(rows, neg):
                    sp.dma_start(dst.bitcast(F32), src[0:heads_of(b) * KT, :].bitcast(F32)).then_inc(shift_loaded[b], 16)

            def turn_sums(b, img, summed):
                sp.wait_ge(act_done, summed + 2)
                for h in range(heads_of(b)):
                    sp.dma_start(sums_dram[b][h:h + 1, :], rb[DH * h:DH * h + 1, :]).then_inc(sums_out[b], 16)
                sp.wait_ge(sums_out[b], 16 * heads_of(b) * (img + 1))
                sp.dma_start(compact[b][:, :].rearrange("p (h e) -> p h e", h=heads_of(b)),
                             sums_dram[b].rearrange("h (p e) -> p h e", p=C)).then_inc(sums_in[b], 16)

            def spread_reciprocals(b, img):
                sp.wait_ge(recip_done[b], img + 1)
                sp.dma_start(recip_dram[b].rearrange("h (p e) -> p h e", p=C),
                             compact[b][:, :].rearrange("p (h e) -> p h e", h=heads_of(b))).then_inc(recip_out[b], 16)
                sp.wait_ge(recip_out[b], 16 * (img + 1))
                rows = C // heads_of(b)
                for h in range(heads_of(b)):
                    sp.dma_start(rb[rows * h:rows * (h + 1), :],
                                 recip_dram[b][h:h + 1, :].to_broadcast([rows, N])).then_inc(rb_loaded[b], 16)

            def run(steps, at, parity, i, y):
                for s in steps:
                    name, img, arg = s
                    b, par = int(name[-1]), parity_of(s, parity)
                    name = name[:-1]
                    if name in ("splitq", "splitk"):
                        if b == 0:
                            stack(img, par, 0 if name == "splitq" else 1)
                    elif name == "shift":
                        load_shift(b, img, par, at)
                    elif name == "recip":
                        turn_sums(b, img, score_position(i, y, f"sums{b}"))
                        spread_reciprocals(b, img)
                    elif name == "proj" and arg == 1:
                        if b == 1:
                            sp.wait_ge(work_free, at + 1)
                            sp.dma_start(out_dram[img], x1[:, par, :]).then_inc(stored, 16)
                        elif not (isinstance(img, int) and img + 2 >= images):
                            sp.wait_ge(work_free, at + 1)
                            sp.dma_start(xin[:, par, :], x_dram[img + 2]).then_inc(x_loaded, 16)
                    at = at + uses_work(s)

            run(START, 0, 1, 0, False)

            def body(i, parity):
                for y in (False, True):
                    run((work_steps_y if y else work_steps_x)(i, images), work_before(i, y), parity, i, y)

            bodies(sp, body)
            for i in (images, images + 1):
                run(work_steps_x(i, images), work_before(i, False), i % 2, i, False)
            sp.wait_ge(stored, 16 * images)

        @block.gpsimd
        def _(pool):
            fills = [(ones[:, :].bitcast(F32), 1.0), (minus_half[:, :], -0.5), (shift1[:, :].bitcast(F32), 0.0)]
            fills += [(ks[p][SPLIT:C, :, :].bitcast(F32), 1.0) for p in range(2)]
            for n, (dst, value) in enumerate(fills):
                if n:
                    pool.wait_ge(pool_ready, n)
                pool.memset(dst, value).then_inc(pool_ready, 1)

            def rstd(b, img):
                pool.wait_ge(gn_chain[b], GN_CHAIN * img + 6)
                pool.tensor_tensor(gn[b][:, RSTD:RSTD + 1], gn[b][:, VAREPS:VAREPS + 1], minus_half[:, :],
                                   ALU.pow).then_inc(rstd_done[b], 1)

            def add(i, parity, y, kt, h):
                pool.wait_ge(act_done, exp_position(i, y, kt, h) + 2)
                n = kt - 1 if y else HEADS * (kt - 1) + h
                total = sum1[:, :] if y else sum0[:, h, :]
                if kt == 1:
                    pool.wait_ge(pv_done, pv_before(i, y) + 1)
                else:
                    pool.wait_ge(pool_added, pool_adds_before(i, y) + (kt - 2 if y else POOL_HEADS * (kt - 2) + h) + 1)
                pool.tensor_tensor(total, total, probs[:, ring_slot(i, parity, y, n), :],
                                   ALU.add).then_inc(pool_added, 1)

            pool.wait_ge(pool_ready, len(fills))
            rstd(0, 0)

            def key_tile(gaps, per, name):
                return [any(s[0] == name for s in steps) for steps in gaps].index(True) // per

            def body(i, parity):
                has_next = present(i + 1, images)
                at = max(1, min(2, key_tile(gaps_x(i, images), X_GAPS, "norm0") - 1)) if has_next else None
                for kt in range(1, KT):
                    for h in range(POOL_HEADS):
                        add(i, parity, False, kt, h)
                    if kt == at:
                        rstd(0, i + 1)
                at = max(0, min(3, key_tile(gaps_y(i, images), Y_GAPS, "norm1") - 1))
                for kt in range(KT):
                    if kt and present(i - 1, images):
                        add(i, parity, True, kt, 0)
                    if kt == at:
                        rstd(1, i)

            bodies(pool, body)
            for kt in range(1, KT):
                add(images, 0, True, kt, 0)

        @block.scalar
        def _(act):
            def exp(i, parity, y, kt, h, at):
                n = kt if y else HEADS * kt + h
                if kt == 0:
                    dst = sum1[:, :] if y else sum0[:, h, :]
                    if y:
                        act.wait_ge(stacked, 16 * STACK_DMAS * (images if isinstance(i, int) and i + 2 > images else i + 2))
                else:
                    r = n - 1 if y else n - HEADS
                    free_probs(i, y, r)
                    dst = probs[:, ring_slot(i, parity, y, r), :]
                for half in range(2):
                    act.wait_ge(act_full, at + half + 1)
                    act.activation(dst[:, halves(half)], score[half][:, :], ACT.Exp, scale=SCALE).then_inc(act_done, 1)

            def free_probs(i, y, r):
                u = r - P_RING
                per_x = (KT - 1) * HEADS
                if y and u < 0 and not (isinstance(i, int) and i >= images):
                    y, u = False, u + per_x
                elif u < 0:
                    if isinstance(i, int) and i <= 1:
                        if i == 0:
                            return
                        i, y, u = 0, False, u + per_x
                    else:
                        i, y, u = i - 1, True, u + KT - 1
                        if u < 0:
                            y, u = False, u + per_x
                if y:
                    act.wait_ge(pv_done, pv_before(i, True) + u + 2)
                    act.wait_ge(pool_added, pool_adds_before(i, True) + u + 1)
                    return
                kt, h = u // HEADS + 1, u % HEADS
                act.wait_ge(pv_done, pv_before(i, False) + kt + 1)
                if h < POOL_HEADS:
                    act.wait_ge(pool_added, pool_adds_before(i, False) + POOL_HEADS * (kt - 1) + h + 1)
                else:
                    act.wait_ge(dve_added, DVE_HEADS * ((KT - 1) * i + kt - 1) + h - POOL_HEADS + 1)

            def save(i, y):
                act.wait_ge(pv_done, pv_before(i, y) + KT)
                if y:
                    y_too = not (isinstance(i, int) and i >= images)
                    act.wait_ge(work_full, work_position(i, y_too, "proj0" if y_too else "proj1", 1) + 1)
                elif present(i - 2, images):
                    act.wait_ge(work_full, work_position(i, False, "proj1", 1) + 1)
                act.copy(mix[:, :], acc[:, :]).then_inc(saved, 1)

            def beside(s, par, at):
                name, img, _ = s
                b = int(name[-1])
                name = name[:-1]
                if name in ("q", "k"):
                    which = 0 if name == "q" else 1
                    hi = (part, part1)[b][2 * which]
                    full = part[2 * which + 1][:, :].bitcast(F32)
                    if b == 1:
                        act.wait_ge(stacked, 16 * STACK_DMAS * (images if isinstance(img, int) and img + 2 > images else img + 2))
                    elif not (isinstance(img, int) and img == 0):
                        act.wait_ge(stacked, 16 * STACK_DMAS * img)
                        if not (isinstance(img, int) and img < 2):
                            act.wait_ge(split_done[1], 2 * (img - 2) + 2)
                elif name == "sums":
                    if b == 0 and not (isinstance(img, int) and img < 2):
                        act.wait_ge(scaled[1], img - 1)
                    if b == 1:
                        both = isinstance(img, int) and img + 2 > images
                        act.wait_ge(scaled[0], images if both else img + 2)
                        if both:
                            act.wait_ge(scaled[1], img)
                elif name == "v":
                    if b == 0 and not (isinstance(img, int) and img < 2):
                        act.wait_ge(pv_done, pv_before(img - 2, False) + KT)
                    if b == 1 and not (isinstance(img, int) and img == 0):
                        act.wait_ge(pv_done, pv_before(img, True) + KT)
                for half in range(2):
                    act.wait_ge(act_full, at + half + 1)
                    if name in ("q", "k"):
                        bias = vec(b, BQ if which == 0 else BK)
                        act.activation(hi[:, halves(half)], score[half][:, :], ACT.Identity, bias=bias)
                        act.activation(full[:, halves(half)], score[half][:, :], ACT.Identity, bias=bias).then_inc(act_done, 1)
                    elif name == "v":
                        dst = v0[:, par, :, :] if b == 0 else v1[:, :, :]
                        act.copy(dst[:, 4 * half:4 * half + 4, :].rearrange("p t n -> p (t n)"),
                                 score[half][:, :]).then_inc(act_done, 1)
                    else:
                        act.copy(rb[:, halves(half)], score[half][:, :]).then_inc(act_done, 1)

            at = 0
            act.wait_ge(const_loaded, 48)
            for s in START:
                if s[0][:-1] in SCORE:
                    beside(s, 0, at)
                    at += 2

            def run(i, parity, y):
                at = scores_before(i, y)
                for s in (score_steps_y if y else score_steps_x)(i, images):
                    if s[0][:-1] == "exp":
                        kt, h = s[2]
                        exp(i, parity, y, kt, h, at)
                        if y and kt == 0 and present(i, images):
                            save(i, False)
                        elif not y and (kt, h) == (0, HEADS - 1) and present(i - 2, images):
                            save(i - 1, True)
                    else:
                        beside(s, parity_of(s, parity), at)
                    at = at + 2

            def body(i, parity):
                run(i, parity, False)
                if isinstance(i, int) and i == 0:
                    save(0, False)
                run(i, parity, True)

            bodies(act, body)
            save(images - 1, True)
            run(images, 0, False)
            run(images, 0, True)
            save(images, True)
            run(images + 1, 1, False)

        @block.vector
        def _(dve):
            def group_norm(b, name, img, par, at, bank):
                chain, g, base = gn_chain[b], gn[b], GN_CHAIN * img
                src = xin[:, par, :] if b == 0 else x1[:, par, :]

                def col(n):
                    return g[:, n:n + 1]

                if name == "stats":
                    if b == 0:
                        dve.wait_ge(x_loaded, 16 * (img + 1))
                    else:
                        dve.wait_ge(x1_done, 2 * (img + 1))
                    for h in range(2):
                        dve.bn_stats(stats[b][:, h, :], src[:, halves(h)]).then_inc(chain, 1)
                    dve.wait_ge(chain, base + 2)
                    dve.tensor_copy(col(GAIN), stats[b][:, 0, 0:1])
                    dve.bn_aggr(mv[b][:, :], stats[b][:, :, :]).then_inc(chain, 1)
                elif name == "mean":
                    dve.wait_ge(work_full, at + 1)
                    dve.tensor_tensor(col(DIFF), mv[b][:, 0:1], work[bank][:, 0:1], ALU.subtract).then_inc(chain, 1)
                    dve.tensor_copy(col(GMEAN), work[bank][:, 0:1]).then_inc(work_free, 1)
                    dve.wait_ge(chain, base + 4)
                    dve.scalar_tensor_tensor(out=col(VARIN), in0=col(DIFF), scalar=col(DIFF), in1=mv[b][:, 1:2],
                                             op0=ALU.mult, op1=ALU.add).then_inc(chain, 1)
                elif name == "var":
                    dve.wait_ge(work_full, at + 1)
                    dve.tensor_scalar(col(VAREPS), work[bank][:, 0:1], EPS[b], None, ALU.add).then_inc(chain, 1)
                    dve.wait_ge(chain, base + 6)
                    dve.tensor_copy(col(MG), work[bank][:, 0:1]).then_inc(work_free, 1)
                elif name == "norm":
                    dve.wait_ge(rstd_done[b], img + 1)
                    dve.tensor_tensor(col(GAIN), col(RSTD), vec(b, GAMMA), ALU.mult).then_inc(chain, 1)
                    dve.wait_ge(chain, base + 7)
                    dve.tensor_tensor(col(MG), col(GMEAN), col(GAIN), ALU.mult).then_inc(chain, 1)
                    dve.wait_ge(chain, base + 8)
                    dve.tensor_tensor(col(OFFSET), vec(b, BETA), col(MG), ALU.subtract).then_inc(chain, 1)
                    dve.wait_ge(chain, base + 9)
                    if b == 0 and present(img - 2, images):
                        dve.wait_ge(act_full, score_position(img - 1, False, "v1") + 2)
                    if b == 1 and present(img + 1, images):
                        dve.wait_ge(act_full, score_position(img, False, "v0") + 2)
                    dve.tensor_scalar(xh[:, :], src, col(GAIN), col(OFFSET), ALU.mult, ALU.add).then_inc(chain, 1)

            def split(b, which, img, computed):
                hi = (part, part1)[b][2 * which][:, :].bitcast(F32)
                full = part[2 * which + 1][:, :].bitcast(F32)
                dve.wait_ge(act_done, computed + 2)
                if b == 1 and which == 0 and present(img - 1, images):
                    dve.wait_ge(act_full, exp_position(img, True, KT - 1) + 2)
                dve.tensor_tensor((part, part1)[b][2 * which + 1][:, :], full, hi, ALU.subtract).then_inc(split_done[b], 1)

            def add(i, parity, kt):
                for n, h in enumerate(range(POOL_HEADS, HEADS)):
                    dve.wait_ge(act_done, exp_position(i, False, kt, h) + 2)
                    if kt == 1:
                        dve.wait_ge(pv_done, pv_before(i, False) + 1)
                    else:
                        dve.wait_ge(dve_added, DVE_HEADS * ((KT - 1) * i + kt - 2) + n + 1)
                    dve.tensor_tensor(sum0[:, h, :], sum0[:, h, :],
                                      probs[:, ring_slot(i, parity, False, HEADS * (kt - 1) + h), :],
                                      ALU.add).then_inc(dve_added, 1)

            def step(s, par, at, bank, i, y):
                name, img, arg = s
                b = int(name[-1])
                name = name[:-1]
                if name in ("stats", "mean", "var", "norm"):
                    group_norm(b, name, img, par, at, bank)
                elif name in ("splitq", "splitk"):
                    if i is None:
                        computed = 0 if name == "splitq" else 2
                    else:
                        computed = score_position(i, y, name[-1] + str(b))
                    split(b, 0 if name == "splitq" else 1, img, computed)
                elif name == "add":
                    add(img, par, KT - 1)
                elif name == "max":
                    dve.wait_ge(work_full, at + 1)
                    dve.tensor_reduce(halfmax[b][:, arg // 2, arg % 2:arg % 2 + 1], work[bank][:, :], AX.X,
                                      ALU.max).then_inc(work_free, 1)
                elif name == "gather":
                    dve.wait_ge(work_free, at)
                    dve.tensor_reduce(rowmax[b][:, :], halfmax[b][:, :, :], AX.X, ALU.max).then_inc(rowmax_done[b], 1)
                elif name == "shift":
                    dve.wait_ge(work_full, at + 1)
                    rows = heads_of(b) * KT
                    src = work[bank][0:rows, 0:C]
                    neg_hi, neg_lo = (n[0:rows, :] for n in neg)
                    if b == 1:
                        dve.wait_ge(shift_loaded[0], 32 * (images if isinstance(img, int) and img + 2 > images else img + 2))
                    elif present(img - 2, images):
                        dve.wait_ge(shift_loaded[1], 32 * (img - 1))
                    elif img > 0:
                        dve.wait_ge(shift_loaded[0], 32 * img)
                    dve.tensor_scalar(neg_hi, src, -1.0, None, ALU.mult).then_inc(neg_done[b], 1)
                    dve.wait_ge(neg_done[b], img + 1)
                    dve.scalar_tensor_tensor(out=neg_lo, in0=src, scalar=-1.0, in1=neg_hi.bitcast(F32),
                                             op0=ALU.mult, op1=ALU.subtract).then_inc(work_free, 1)
                elif name == "recip":
                    dve.wait_ge(sums_in[b], 16 * (img + 1))
                    dve.reciprocal(compact[b][:, :], compact[b][:, :]).then_inc(recip_done[b], 1)
                elif name == "scale":
                    dve.wait_ge(rb_loaded[b], 16 * heads_of(b) * (img + 1))
                    dve.wait_ge(saved, saved_before(img + b, b == 1) + 1)
                    dve.tensor_tensor(mix[:, :], mix[:, :], rb[:, :], ALU.mult).then_inc(scaled[b], 1)
                elif name == "proj":
                    dve.wait_ge(work_full, at + 1)
                    dst = x1[:, par, halves(arg)]
                    if b == 0 and arg == 0 and present(img - 2, images):
                        dve.wait_ge(stored, 16 * (img - 1))
                    res = xin[:, par, halves(arg)] if b == 0 else dst
                    dve.scalar_tensor_tensor(out=dst, in0=work[bank][:, :], scalar=proj_bias[:, b:b + 1], in1=res,
                                             op0=ALU.add, op1=ALU.add).then_inc(work_free, 1)
                    if b == 0:
                        dve.wait_ge(work_free, at + 1)
                        dve.tensor_scalar(dst, dst, math.sqrt(0.5), None, ALU.mult).then_inc(x1_done, 1)

            dve.wait_ge(const_loaded, 48)
            for b in range(2):
                dve.wait_ge(bias_ready, b + 1)
                dve.tensor_tensor(proj_bias[:, b:b + 1], acc[:, HALF * b:HALF * b + 1], vec(b, BP),
                                  ALU.add).then_inc(bias_added, 1)
            dve.wait_ge(bias_added, 2)

            def run(steps, at, bank, parity, i, y):
                for s in steps:
                    step(s, parity_of(s, parity), at, bank, i, y)
                    if uses_work(s):
                        at, bank = at + 1, (bank + 1) % BANKS
                return at, bank

            run(START, 0, 0, 1, None, False)

            def body(i, parity):
                at, bank = work_before(i, False), first_bank(i, parity)
                for g, steps in enumerate(gaps_x(i, images)):
                    at, bank = run(steps, at, bank, parity, i, False)
                    if g % X_GAPS == X_GAPS - 1 and g // X_GAPS >= 2:
                        add(i, parity, g // X_GAPS - 1)
                for steps in gaps_y(i, images):
                    at, bank = run(steps, at, bank, parity, i, True)

            bodies(dve, body)
            for i in (images, images + 1):
                run(work_steps_x(i, images), work_before(i, False), first_bank(i, i % 2), i % 2, i, False)

        @block.tensor
        def _(pe):
            def work_step(s, par, at, bank):
                name, img, arg = s
                b = int(name[-1])
                name = name[:-1]
                out_bank = work[bank]
                if not (isinstance(at, int) and at < BANKS):
                    pe.wait_ge(work_free, at - BANKS + 1)
                if name == "mean":
                    pe.wait_ge(gn_chain[b], GN_CHAIN * img + 3)
                    mm = pe.matmul(out_bank[:, 0:1], consts[:, 1 + b, :], mv[b][:, 0:1], start=True, stop=True)
                elif name == "var":
                    pe.wait_ge(gn_chain[b], GN_CHAIN * img + 5)
                    mm = pe.matmul(out_bank[:, 0:1], consts[:, 1 + b, :], gn[b][:, VARIN:VARIN + 1], start=True, stop=True)
                elif name == "max":
                    t, half = arg // 2, arg % 2
                    if b == 0:
                        h, t = t // KT, t % KT
                        if arg == 0:
                            pe.wait_ge(stacked, 16 * STACK_DMAS * (img + 1))
                        mm = pe.matmul(out_bank[:, :], qs[par][0:SPLIT, h, tile(t)], ks[par][0:SPLIT, h, halves(half)],
                                       start=True, stop=True)
                    else:
                        if arg == 0:
                            pe.wait_ge(act_done, score_position(img + 1, False, "k1") + 2)
                        mm = pe.matmul(out_bank[:, :], part1[0][:, tile(t)], part1[2][:, halves(half)], start=True, stop=True)
                elif name == "shift":
                    pe.wait_ge(rowmax_done[b], img + 1)
                    mm = pe.transpose(out_bank[0:heads_of(b) * KT, 0:C], rowmax[b][:, :], identity)
                elif name == "proj":
                    pe.wait_ge(scaled[b], img + 1)
                    mm = pe.matmul(out_bank[:, :], w(b, WP), mix[:, halves(arg)], start=True, stop=True)
                mm.then_inc(work_full, 1)

            def score_bank(at, half):
                if not (isinstance(at, int) and at + half < 2):
                    pe.wait_ge(act_done, at + half - 1)
                return score[half]

            def beside(s, par, at, i):
                name, img, _ = s
                b = int(name[-1])
                name = name[:-1]
                if name in ("q", "k", "v"):
                    pe.wait_ge(gn_chain[b], GN_CHAIN * img + 10)
                elif b == 0:
                    pe.wait_ge(pool_added, pool_adds_before(img, False) + (KT - 1) * POOL_HEADS)
                    pe.wait_ge(dve_added, DVE_HEADS * (KT - 1) * (img + 1))
                else:
                    pe.wait_ge(pool_added, pool_adds_before(img + 1, True) + KT - 1)
                for half in range(2):
                    dst = score_bank(at, half)
                    if name in ("q", "k"):
                        mm = pe.matmul(dst[:, :], w(b, WQ if name == "q" else WK), xh[:, halves(half)], start=True, stop=True)
                    elif name == "v":
                        for t in range(4):
                            mm = pe.matmul(dst[:, tile(t)], xh[:, tile(4 * half + t)], w(b, WV), start=True, stop=True)
                    elif b == 0:
                        for h in range(HEADS):
                            mm = pe.matmul(dst[head(h), :], ones[:, 0:DH].bitcast(F32), sum0[:, h, halves(half)], start=True,
                                           stop=True, tile_position=(0, DH * h))
                    else:
                        mm = pe.matmul(dst[:, :], ones[:, :].bitcast(F32), sum1[:, halves(half)], start=True, stop=True)
                    mm.then_inc(act_full, 1)

            def scores0(i, parity, kt, h, half, at):
                if kt == 0 and h == 0 and half == 0:
                    pe.wait_ge(shift_loaded[0], 32 * (i + 1))
                pe.matmul(score_bank(at, half)[:, :], ks[parity][0:SPLIT + SHIFT, h, tile(kt)],
                          qs[parity][0:SPLIT + SHIFT, h, halves(half)], start=True, stop=True).then_inc(act_full, 1)

            def scores1(i, kt, half, at):
                if kt == 0 and half == 0:
                    pe.wait_ge(shift_loaded[1], 32 * i)
                    pe.wait_ge(split_done[1], 2 * i)
                q_hi, q_lo, k_hi, k_lo = part1
                dst = score_bank(at, half)[:, :]
                pe.matmul(dst, k_hi[:, tile(kt)], q_hi[:, halves(half)], start=True, stop=False)
                pe.matmul(dst, k_hi[:, tile(kt)], q_lo[:, halves(half)], start=False, stop=False)
                pe.matmul(dst, k_lo[:, tile(kt)], q_hi[:, halves(half)], start=False, stop=False)
                pe.matmul(dst, ones[:, :], shift1[:, halves(half)], start=False, stop=True).then_inc(act_full, 1)

            def pv(i, parity, y, kt, half):
                if half == 0:
                    pe.wait_ge(act_done, exp_position(i, y, kt, 0 if y else HEADS - 1) + 2)
                    if kt == 0 and not (isinstance(i, int) and i == 0):
                        pe.wait_ge(saved, saved_before(i, y))
                for h in range(1 if y else HEADS):
                    if y:
                        dst, v = acc[:, halves(half)], v1[:, kt, :]
                        src = sum1[:, halves(half)] if kt == 0 else probs[:, ring_slot(i, parity, True, kt - 1), halves(half)]
                        where = None
                    else:
                        dst, v = acc[head(h), halves(half)], v0[:, parity, kt, head(h)]
                        src = sum0[:, h, halves(half)] if kt == 0 else \
                            probs[:, ring_slot(i, parity, False, HEADS * (kt - 1) + h), halves(half)]
                        where = (0, DH * h)
                    mm = pe.matmul(dst, v, src, start=kt == 0, stop=kt == KT - 1, tile_position=where)
                if half == 1:
                    mm.then_inc(pv_done, 1)

            pe.wait_ge(const_loaded, 48)
            for b in range(2):
                pe.matmul(acc[:, HALF * b:HALF * b + 1], w(b, WP), vec(b, BV), start=True, stop=True).then_inc(bias_ready, 1)
            pe.wait_ge(bias_added, 2)
            pe.wait_ge(pool_ready, 5)

            def run(steps, at, bank, parity):
                for s in steps:
                    if uses_work(s):
                        work_step(s, parity_of(s, parity), at, bank)
                        at, bank = at + 1, (bank + 1) % BANKS
                return at, bank

            at, bank, score_at = 0, 0, 0
            for s in START:
                if s[0][:-1] in SCORE:
                    beside(s, 0, score_at, 0)
                    score_at += 2
                else:
                    at, bank = run([s], at, bank, 1)

            def beside_after(table, n, i, parity, y):
                for name, ahead, at in table:
                    if at == n and present(i + ahead, images):
                        s = (name, i + ahead, None)
                        beside(s, parity_of(s, parity), score_position(i, y, name), i)

            def body_x(i, parity, at, bank):
                gaps = gaps_x(i, images)
                for kt in range(KT):
                    if kt:
                        before = (i, parity, False, kt - 1)
                    elif present(i - 2, images):
                        before = (i - 1, 1 - parity, True, KT - 1)
                    else:
                        before = None
                    own = gaps[X_GAPS * kt:X_GAPS * (kt + 1)]
                    for h in range(HEADS):
                        n = exp_position(i, False, kt, h)
                        scores0(i, parity, kt, h, 0, n)
                        if h % 2 == 0:
                            at, bank = run(own.pop(0), at, bank, parity)
                        elif before:
                            pv(*before, h // 2)
                        scores0(i, parity, kt, h, 1, n)
                        beside_after(BESIDE_X, HEADS * kt + h, i, parity, False)
                        at, bank = run(own.pop(0), at, bank, parity)
                return at, bank

            def body_y(i, parity, at, bank):
                gaps = gaps_y(i, images)
                for kt in range(KT):
                    own = gaps[Y_GAPS * kt:Y_GAPS * (kt + 1)]
                    if kt:
                        before = (i, parity, True, kt - 1)
                    else:
                        before = (i, parity, False, KT - 1) if present(i, images) else None
                    for half in range(2):
                        if present(i - 1, images):
                            scores1(i, kt, half, exp_position(i, True, kt))
                        at, bank = run(own.pop(0), at, bank, parity)
                    beside_after(BESIDE_Y, kt, i, parity, True)
                    for half in range(2):
                        if before and (present(i - 1, images) or kt == 0):
                            pv(*before, half)
                        at, bank = run(own.pop(0), at, bank, parity)
                return at, bank

            def body(i, parity):
                body_y(i, parity, *body_x(i, parity, work_before(i, False), first_bank(i, parity)))

            bodies(pe, body)
            for half in range(2):
                pv(images - 1, 1, True, KT - 1, half)
            for n in range(KT * HEADS):
                beside_after(BESIDE_X, n, images, 0, False)
            run(work_steps_x(images, images), work_before(images, False), first_bank(images, 0), 0)
            body_y(images, 0, work_before(images, True), 0)
            for half in range(2):
                pv(images, 0, True, KT - 1, half)
            for n in range(KT * HEADS):
                beside_after(BESIDE_X, n, images + 1, 1, False)
            run(work_steps_x(images + 1, images), work_before(images + 1, False), first_bank(images + 1, 1), 1)


def kernel(**inputs):
    import numpy as np
    import concourse.bacc as bacc
    from concourse.bass_utils import run_bass_kernel_spmd as run

    a = {k: np.ascontiguousarray(v) for k, v in inputs.items()}
    wq1, wk1, wv1 = a["L1_conv_qkv_w"].reshape(3, C, C)
    weights = np.ascontiguousarray(np.stack(
        [a["L0_conv_Wq"], a["L0_conv_Wk"], a["L0_conv_Wv"], a["L0_conv_Wp"],
         wq1.T, wk1.T, wv1.T, a["L1_conv_proj_w"].T], axis=1))
    bq1, bk1, bv1 = a["L1_conv_qkv_b"].reshape(3, C)
    vectors = np.ascontiguousarray(np.stack(
        [a["L0_conv_gn_scale"], a["L0_conv_gn_bias"], a["L0_conv_bq"], a["L0_conv_bk"], a["L0_conv_bv"],
         a["L0_conv_bp"], a["L1_conv_gn_w"], a["L1_conv_gn_b"], bq1, bk1, bv1, a["L1_conv_proj_b"]], axis=1))
    channel = np.arange(C)
    constants = np.stack(
        [np.eye(C)] + [(channel[:, None] // g == channel[None, :] // g) / g for g in (C // 32, C // 8)],
        axis=1).astype(np.float32)
    arrays = {"x_dram": a["x"], "weights_dram": weights, "vectors_dram": vectors,
              "constants_dram": np.ascontiguousarray(constants)}

    nc = bacc.Bacc("TRN2", target_bir_lowering=False, num_devices=1)
    args = [nc.dram_tensor(n, v.shape, mybir.dt.from_np(v.dtype), kind="ExternalInput").ap() for n, v in arrays.items()]
    out = nc.dram_tensor("out_0_dram", a["x"].shape, F32, kind="ExternalOutput").ap()
    bass_two_attention_blocks(nc, *args, out)
    return run(nc, [arrays], core_ids=[0]).results[0]["out_0_dram"]
```

```python
from contextlib import ExitStack
import math

import concourse.bass as bass
from concourse import mybir

F32 = mybir.dt.float32
F32R = mybir.dt.float32r
ALU = mybir.AluOpType
ACT = mybir.ActivationFunctionType
AX = mybir.AxisListType

C = 128
N = 1024
HALF = 512
KT = N // C
HEADS = 4
DH = C // HEADS
SPLIT = 3 * DH
SHIFT = 2
NVEC = 12
P_RING = 10
SCALE = 1.0 / math.sqrt(C)
EPS = (1e-6, 1e-5)

BANKS = 3
SCORE_BANKS = 3
WQ, WK, WV, WP = range(4)
GAMMA, BETA, BQ, BK, BV, BP = range(6)

MAXES_IN_X, FIRST_MAXES_IN_X = 18, 30

X_GAPS, Y_GAPS = 6, 4

BESIDE_X = [("sums1", -2, 3), ("q1", -1, 0), ("k1", -1, 1), ("v1", -1, 7), ("q0", 1, 8), ("k0", 1, 11),
            ("v0", 1, 16)]
BESIDE_Y = [("sums0", 0, 1)]


def gap_x(name):
    n = [n for step, _, n in BESIDE_X if step == name][0]
    kt, h = divmod(n, HEADS)
    return X_GAPS * kt + h + h // 2 + 1 - h % 2


PLACE_X = [("stats0", 1, 0, 4), ("mean0", 1, 0, 4), ("splitq1", -1, 0, 4), ("splitk1", -1, 0, gap_x("k1") + 5),
           ("var0", 1, 0, 6), ("norm0", 1, 0, 10), ("recip1", -2, 0, 13), ("splitq0", 1, 0, gap_x("q0") + 1),
           ("splitk0", 1, 0, gap_x("k0") + 5), ("scale1", -2, 0, 25), ("proj1", -2, 0, 26), ("proj1", -2, 1, 30),
           ("gather1", -1, 0, 30), ("shift1", -1, 0, 36)]
PLACE_Y = [("add0", 0, 0, 0), ("recip0", 0, 0, 9), ("scale0", 0, 0, 18), ("proj0", 0, 0, 20),
           ("proj0", 0, 1, 20), ("stats1", 0, 0, 20), ("mean1", 0, 0, 24), ("var1", 0, 0, 25),
           ("norm1", 0, 0, 27), ("gather0", 1, 0, 27), ("shift0", 1, 0, 27)]


def maxes_in_x(i):
    return FIRST_MAXES_IN_X if isinstance(i, int) and i == 0 else MAXES_IN_X


def maxima_x(i):
    later = 8 if isinstance(i, int) and i == 0 else 13
    return [("max1", -1, range(2 * KT), gap_x("k1") + 11, 30),
            ("max0", 1, range(maxes_in_x(i)), gap_x("k0") + later, X_GAPS * KT)]


def maxima_y(i):
    return [("max0", 1, range(maxes_in_x(i), 2 * KT * HEADS), 0, 26)]


WEIGHT = {"stats": 2, "mean": 1, "var": 1, "max": 1, "norm": 1, "splitq": 3, "splitk": 3, "recip": 0,
          "scale": 2, "gather": 0, "shift": 1, "proj": 1, "add": 3}


def present(image, images):
    return not isinstance(image, int) or 0 <= image < images


def spread(places, maxima, gaps, i, images):
    fixed, at = [[] for _ in range(gaps)], 0
    for name, ahead, arg, gap in places:
        at = max(at, gap)
        if present(i + ahead, images):
            fixed[at].append((name, i + ahead, arg))
    out = [[] for _ in range(gaps)]

    def weight(steps):
        return sum(WEIGHT[s[0][:-1]] for s in steps)

    for name, ahead, numbers, first, end in maxima:
        if not present(i + ahead, images):
            continue
        rate = 0.0
        while True:
            left, placed, total = list(numbers), [[] for _ in range(gaps)], 0.0
            for g in range(first, end):
                total += weight(fixed[g]) + weight(out[g])
                while left and total < rate * (g - first + 1):
                    placed[g].append((name, i + ahead, left.pop(0)))
                    total += 1
            if not left:
                break
            rate += 0.02
        out = [a + b for a, b in zip(out, placed)]
    return [m + f for m, f in zip(out, fixed)]


def gaps_x(i, images):
    return spread(PLACE_X, maxima_x(i), X_GAPS * KT, i, images)


def gaps_y(i, images):
    return spread(PLACE_Y, maxima_y(i), Y_GAPS * KT, i, images)


def work_steps_x(i, images):
    steps = sum(gaps_x(i, images), [])
    if isinstance(i, int) and i >= images:
        steps.sort(key=lambda s: s[0] in ("scale1", "proj1"))
    return steps


def work_steps_y(i, images):
    return sum(gaps_y(i, images), [])


def score_steps_x(i, images):
    steps = []
    for n in range(KT * HEADS):
        if present(i, images):
            steps.append(("exp0", i, divmod(n, HEADS)))
        steps += [(name, i + ahead, None) for name, ahead, at in BESIDE_X if at == n and present(i + ahead, images)]
    return steps


def score_steps_y(i, images):
    steps = []
    for kt in range(KT):
        if present(i - 1, images):
            steps.append(("exp1", i - 1, (kt, 0)))
        steps += [(name, i + ahead, None) for name, ahead, at in BESIDE_Y if at == kt and present(i + ahead, images)]
    return steps


START = ([("stats0", 0, 0), ("mean0", 0, 0), ("var0", 0, 0), ("norm0", 0, 0), ("q0", 0, None),
          ("splitq0", 0, 0), ("k0", 0, None), ("splitk0", 0, 0), ("v0", 0, None)]
         + [("max0", 0, n) for n in range(2 * KT * HEADS)] + [("gather0", 0, 0), ("shift0", 0, 0)])

WORK = ("mean", "var", "max", "shift", "proj")
SCORE = ("exp", "sums", "q", "k", "v")


def uses_work(step):
    return step[0][:-1] in WORK


def work_count(steps):
    return sum(map(uses_work, steps))


def score_count(steps):
    return 2 * sum(s[0][:-1] in SCORE for s in steps)


def bass_two_attention_blocks(nc, x, weights, vectors, constants, out):
    images = x.shape[0]
    x_dram = x.rearrange("b c h w -> b c (h w)")
    out_dram = out.rearrange("b c h w -> b c (h w)")

    def counter(count, steps_x, steps_y, start):
        per_body = count(steps_x(5, images)) + count(steps_y(5, images))

        def before_x(i):
            if isinstance(i, int) and (i < 2 or i >= images):
                at, first = (start, 0) if i < 2 else (before_x(images - 1), images - 1)
                for n in range(first, i):
                    at += count(steps_x(n, images)) + count(steps_y(n, images))
                return at
            return before_x(1) + count(steps_x(1, images)) + count(steps_y(1, images)) + (i - 2) * per_body

        def before(i, y):
            return before_x(i) + (count(steps_x(i, images)) if y else 0)

        return before, per_body

    work_before, work_per_body = counter(work_count, work_steps_x, work_steps_y, work_count(START))
    scores_before, scores_per_body = counter(score_count, score_steps_x, score_steps_y, score_count(START))

    def score_position(i, y, name, arg=None):
        n = 0
        for s in (score_steps_y if y else score_steps_x)(i, images):
            if (s[0], s[2]) == (name, arg):
                return scores_before(i, y) + 2 * n
            n += 1
        raise KeyError((name, arg))

    def exp_position(i, y, kt, h=0):
        return score_position(i, y, "exp1" if y else "exp0", (kt, h))

    def before_x(i, x_count, y_count):
        return 0 if isinstance(i, int) and i == 0 else (x_count + y_count) * i - y_count

    def before_y(i, x_count, y_count):
        if isinstance(i, int) and i >= images:
            return before_x(i, x_count, y_count)
        return before_x(i, x_count, y_count) + x_count

    def ring_before(i, y):
        return (before_y if y else before_x)(i, (KT - 1) * HEADS, KT - 1)

    def pv_before(i, y):
        return (before_y if y else before_x)(i, KT, KT)

    POOL_HEADS = 3
    DVE_HEADS = HEADS - POOL_HEADS

    def pool_adds_before(i, y):
        return (before_y if y else before_x)(i, (KT - 1) * POOL_HEADS, KT - 1)

    def saved_before(i, y):
        return (before_y if y else before_x)(i, 1, 1)

    def ring_slot(i, parity, y, n):
        j = i if isinstance(i, int) else 2 + parity
        return (ring_before(j, y) + n) % P_RING

    with ExitStack() as ctx:
        def sb(name, shape, dt=F32):
            return ctx.enter_context(nc.sbuf_tensor(name, shape, dt))

        def ps(name, shape, dt=F32):
            return ctx.enter_context(nc.psum_tensor(name, shape, dt))

        def sem(name):
            return ctx.enter_context(nc.semaphore(name))

        wts = sb("wts", [C, 8, C])
        vecs = sb("vecs", [C, NVEC])
        consts = sb("consts", [C, 3, C])
        ones = sb("ones", [C, C], F32R)
        minus_half = sb("minus_half", [C, 1])
        xin = sb("xin", [C, 2, N])
        x1 = sb("x1", [C, 2, N])
        xh = sb("xh", [C, N])
        part = [sb(n, [C, N], F32R) for n in ("q_hi", "q_lo", "k_hi", "k_lo")]
        qs = [sb(f"q_stack{p}", [C, HEADS, N], F32R) for p in range(2)]
        ks = [sb(f"k_stack{p}", [C, HEADS, N], F32R) for p in range(2)]
        part1 = [sb(n, [C, N], F32R) for n in ("q1_hi", "q1_lo", "k1_hi", "k1_lo")]
        shift1 = sb("shift1", [C, N], F32R)
        v0 = sb("v0", [C, 2, KT, C])
        v1 = sb("v1", [C, KT, C])
        probs = sb("probs", [C, P_RING, N])
        sum0 = sb("sum0", [C, HEADS, N])
        sum1 = part[0][:, :].bitcast(F32)
        mix = sb("mix", [C, N])
        rb = sb("rb", [C, N])
        compact = [sb(f"compact{b}", [C, h * KT]) for b, h in ((0, HEADS), (1, 1))]
        halfmax = [sb(f"halfmax{b}", [C, h * KT, 2]) for b, h in ((0, HEADS), (1, 1))]
        rowmax = [sb(f"rowmax{b}", [C, h * KT]) for b, h in ((0, HEADS), (1, 1))]
        neg = [sb(n, [HEADS * KT, C], F32R) for n in ("neg_hi", "neg_lo")]
        stats = [sb(f"stats{b}", [C, 2, 6]) for b in range(2)]
        mv = [sb(f"mv{b}", [C, 2]) for b in range(2)]
        gn = [sb(f"gn{b}", [C, 8]) for b in range(2)]
        proj_bias = sb("proj_bias", [C, 2])
        DIFF, GMEAN, VARIN, VAREPS, RSTD, GAIN, MG, OFFSET = range(8)

        sums_dram = [nc.dram_tensor(f"sums_dram{b}", (h, N), F32).ap() for b, h in ((0, HEADS), (1, 1))]
        recip_dram = [nc.dram_tensor(f"recip_dram{b}", (h, N), F32).ap() for b, h in ((0, HEADS), (1, 1))]

        score = [ps(f"score{n}", [C, HALF]) for n in range(SCORE_BANKS)]
        acc = ps("acc", [C, N])
        work = [ps(f"work{n}", [C, HALF]) for n in range(BANKS)]

        const_loaded = sem("const_loaded")
        pool_ready = sem("pool_ready")
        bias_ready = sem("bias_ready")
        x_loaded = sem("x_loaded")
        work_full = sem("work_full")
        work_free = sem("work_free")
        hi_done = [sem(f"hi_done{b}") for b in range(2)]
        split_done = [sem(f"split_done{b}") for b in range(2)]
        neg_done = [sem(f"neg_done{b}") for b in range(2)]
        bias_added = sem("bias_added")
        gn_chain = [sem(f"gn_chain{b}") for b in range(2)]
        GN_CHAIN = 10
        rstd_done = [sem(f"rstd_done{b}") for b in range(2)]
        stacked = [sem(f"stacked{h}") for h in range(HEADS)]
        STACK_DMAS = 6
        rowmax_done = [sem(f"rowmax_done{b}") for b in range(2)]
        shift_loaded = [sem(f"shift_loaded{b}") for b in range(2)]
        act_full = sem("act_full")
        act_done = sem("act_done")
        pv_done = sem("pv_done")
        pool_added = sem("pool_added")
        dve_added = sem("dve_added")
        saved = sem("saved")
        sums_out = [sem(f"sums_out{b}") for b in range(2)]
        sums_in = [sem(f"sums_in{b}") for b in range(2)]
        recip_done = [sem(f"recip_done{b}") for b in range(2)]
        recip_out = [sem(f"recip_out{b}") for b in range(2)]
        rb_loaded = [sem(f"rb_loaded{b}") for b in range(2)]
        scaled = [sem(f"scaled{b}") for b in range(2)]
        x1_done = sem("x1_done")
        stored = sem("stored")

        def w(b, which):
            return wts[:, 4 * b + which, :]

        def vec(b, which):
            return vecs[:, 6 * b + which:6 * b + which + 1]

        identity = consts[:, 0, :]

        def heads_of(b):
            return HEADS if b == 0 else 1

        def halves(h):
            return slice(HALF * h, HALF * (h + 1))

        def on_the_spot(b, img):
            return b == 1 and isinstance(img, int) and img == images - 1

        def tile(t):
            return slice(C * t, C * (t + 1))

        def head(h):
            return slice(DH * h, DH * (h + 1))

        def work_position(i, y, name, arg=0):
            n = 0
            for s in (work_steps_y if y else work_steps_x)(i, images):
                if (s[0], s[2]) == (name, arg):
                    return work_before(i, y) + n
                n += uses_work(s)
            raise KeyError((name, arg))

        assert scores_per_body % SCORE_BANKS == 0, "a body has to leave the score banks as it found them"

        def score_bank(i, y, name, arg=None):
            return score_position(i if isinstance(i, int) else 2, y, name, arg) % SCORE_BANKS

        assert 2 * work_per_body % BANKS == 0, "an iteration of the loop has to leave the banks as it found them"

        def first_bank(i, parity):
            return work_before(i if isinstance(i, int) else 2 + parity, False) % BANKS

        def parity_of(s, parity):
            name, b = s[0][:-1], int(s[0][-1])
            same = name in ("sums", "recip", "scale", "proj", "add") or (b == 1 and name in ("stats", "mean", "var", "norm"))
            return parity if same else 1 - parity

        def bodies(engine, body):
            body(0, 0)
            body(1, 1)
            with engine.Fori(1, images // 2 - 1) as pair:
                body(2 * pair, 0)
                body(2 * pair + 1, 1)
            body(images - 2, 0)
            body(images - 1, 1)

        block = ctx.enter_context(nc.Block())

        @block.sync
        def _(sp):
            sp.dma_start(xin[:, 0, :], x_dram[0]).then_inc(x_loaded, 16)
            sp.dma_start(wts[:, :, :], weights).then_inc(const_loaded, 16)
            sp.dma_start(vecs[:, :], vectors).then_inc(const_loaded, 16)
            sp.dma_start(consts[:, :, :], constants).then_inc(const_loaded, 16)
            sp.dma_start(xin[:, 1, :], x_dram[1]).then_inc(x_loaded, 16)

            def stack(img, par, which):
                sp.wait_ge(split_done[0], 2 * img + which[-1] + 1)
                for h in range(HEADS):
                    for n in which:
                        hi, lo = part[2 * n:2 * n + 2]
                        for group, src in enumerate((hi, lo, hi) if n == 0 else (hi, hi, lo)):
                            sp.dma_start((qs, ks)[n][par][DH * group:DH * (group + 1), h, :].bitcast(F32),
                                         src[head(h), :].bitcast(F32)).then_inc(stacked[h], 16)

            def load_shift(b, img, par, at):
                if b == 0:
                    rows = [qs[par][SPLIT + n:SPLIT + n + 1, :, :].rearrange("p h (t n) -> p (h t) n", t=KT)
                            for n in range(SHIFT)]
                else:
                    rows = [shift1[n:n + 1, :].rearrange("p (t n) -> p t n", t=KT) for n in range(SHIFT)]
                sp.wait_ge(work_free, at + 1)
                for dst, src in zip(rows, neg):
                    sp.dma_start(dst.bitcast(F32), src[0:heads_of(b) * KT, :].bitcast(F32)).then_inc(shift_loaded[b], 16)

            def turn_sums(b, img, summed):
                sp.wait_ge(act_done, summed + 2)
                for h in range(heads_of(b)):
                    sp.dma_start(sums_dram[b][h:h + 1, :], rb[DH * h:DH * h + 1, :]).then_inc(sums_out[b], 16)
                sp.wait_ge(sums_out[b], 16 * heads_of(b) * (img + 1))
                sp.dma_start(compact[b][:, :].rearrange("p (h e) -> p h e", h=heads_of(b)),
                             sums_dram[b].rearrange("h (p e) -> p h e", p=C)).then_inc(sums_in[b], 16)

            def spread_reciprocals(b, img):
                sp.wait_ge(recip_done[b], img + 1)
                sp.dma_start(recip_dram[b].rearrange("h (p e) -> p h e", p=C),
                             compact[b][:, :].rearrange("p (h e) -> p h e", h=heads_of(b))).then_inc(recip_out[b], 16)
                sp.wait_ge(recip_out[b], 16 * (img + 1))
                rows = C // heads_of(b)
                for h in range(heads_of(b)):
                    sp.dma_start(rb[rows * h:rows * (h + 1), :],
                                 recip_dram[b][h:h + 1, :].to_broadcast([rows, N])).then_inc(rb_loaded[b], 16)

            def run(steps, at, parity, i, y):
                for s in steps:
                    name, img, arg = s
                    b, par = int(name[-1]), parity_of(s, parity)
                    name = name[:-1]
                    if name in ("splitq", "splitk"):
                        first = isinstance(img, int) and img == 0
                        if b == 0 and name == "splitk":
                            stack(img, par, (0, 1) if first else (1,))
                        elif b == 0 and not first:
                            stack(img, par, (0,))
                    elif name == "shift":
                        load_shift(b, img, par, at)
                    elif name == "recip" and not on_the_spot(b, img):
                        turn_sums(b, img, score_position(i, y, f"sums{b}"))
                        spread_reciprocals(b, img)
                    elif name == "proj" and arg == 1:
                        if b == 1:
                            sp.wait_ge(work_free, at + 1)
                            sp.dma_start(out_dram[img], x1[:, par, :]).then_inc(stored, 16)
                        elif not (isinstance(img, int) and img + 2 >= images):
                            sp.wait_ge(work_free, at + 1)
                            sp.dma_start(xin[:, par, :], x_dram[img + 2]).then_inc(x_loaded, 16)
                    at = at + uses_work(s)

            run(START, 0, 1, 0, False)

            def body(i, parity):
                for y in (False, True):
                    run((work_steps_y if y else work_steps_x)(i, images), work_before(i, y), parity, i, y)

            bodies(sp, body)
            for i in (images, images + 1):
                run(work_steps_x(i, images), work_before(i, False), i % 2, i, False)
            sp.wait_ge(stored, 16 * images)

        @block.gpsimd
        def _(pool):
            fills = [(ones[:, :].bitcast(F32), 1.0), (minus_half[:, :], -0.5), (shift1[:, :].bitcast(F32), 0.0)]
            fills += [(ks[p][SPLIT:C, :, :].bitcast(F32), 1.0) for p in range(2)]
            for n, (dst, value) in enumerate(fills):
                if n:
                    pool.wait_ge(pool_ready, n)
                pool.memset(dst, value).then_inc(pool_ready, 1)

            def rstd(b, img):
                pool.wait_ge(gn_chain[b], GN_CHAIN * img + 6)
                pool.tensor_tensor(gn[b][:, RSTD:RSTD + 1], gn[b][:, VAREPS:VAREPS + 1], minus_half[:, :],
                                   ALU.pow).then_inc(rstd_done[b], 1)

            def add(i, parity, y, kt, h):
                pool.wait_ge(act_done, exp_position(i, y, kt, h) + 2)
                n = kt - 1 if y else HEADS * (kt - 1) + h
                total = sum1[:, :] if y else sum0[:, h, :]
                if kt == 1:
                    pool.wait_ge(pv_done, pv_before(i, y) + 1)
                else:
                    pool.wait_ge(pool_added, pool_adds_before(i, y) + (kt - 2 if y else POOL_HEADS * (kt - 2) + h) + 1)
                pool.tensor_tensor(total, total, probs[:, ring_slot(i, parity, y, n), :],
                                   ALU.add).then_inc(pool_added, 1)

            pool.wait_ge(pool_ready, len(fills))
            rstd(0, 0)

            RSTD_AT = 10

            def key_tile(gaps, per, name):
                return [any(s[0] == name for s in steps) for steps in gaps].index(True) // per

            def body(i, parity):
                has_next = present(i + 1, images)
                at = min(RSTD_AT, POOL_HEADS * (key_tile(gaps_x(i, images), X_GAPS, "norm0") - 1)) if has_next else None
                for n in range(POOL_HEADS * (KT - 1)):
                    if n == at:
                        rstd(0, i + 1)
                    add(i, parity, False, n // POOL_HEADS + 1, n % POOL_HEADS)
                at = max(0, min(6, key_tile(gaps_y(i, images), Y_GAPS, "norm1") - 1))
                for kt in range(KT):
                    if kt and present(i - 1, images):
                        add(i, parity, True, kt, 0)
                    if kt == at:
                        rstd(1, i)

            bodies(pool, body)
            for kt in range(1, KT):
                add(images, 0, True, kt, 0)

        @block.scalar
        def _(act):
            def exp(i, parity, y, kt, h, at, bank):
                n = kt if y else HEADS * kt + h
                if kt == 0:
                    dst = sum1[:, :] if y else sum0[:, h, :]
                    if y:
                        for h in range(HEADS):
                            act.wait_ge(stacked[h], 16 * STACK_DMAS * (images if isinstance(i, int) and i + 2 > images else i + 2))
                else:
                    r = n - 1 if y else n - HEADS
                    free_probs(i, y, r)
                    dst = probs[:, ring_slot(i, parity, y, r), :]
                for half in range(2):
                    act.wait_ge(act_full, at + half + 1)
                    act.activation(dst[:, halves(half)], score[(bank + half) % SCORE_BANKS][:, :], ACT.Exp, scale=SCALE).then_inc(act_done, 1)

            def free_probs(i, y, r):
                u = r - P_RING
                per_x = (KT - 1) * HEADS
                if y and u < 0 and not (isinstance(i, int) and i >= images):
                    y, u = False, u + per_x
                elif u < 0:
                    if isinstance(i, int) and i <= 1:
                        if i == 0:
                            return
                        i, y, u = 0, False, u + per_x
                    else:
                        i, y, u = i - 1, True, u + KT - 1
                        if u < 0:
                            y, u = False, u + per_x
                if y:
                    act.wait_ge(pv_done, pv_before(i, True) + u + 2)
                    act.wait_ge(pool_added, pool_adds_before(i, True) + u + 1)
                    return
                kt, h = u // HEADS + 1, u % HEADS
                act.wait_ge(pv_done, pv_before(i, False) + kt + 1)
                if h < POOL_HEADS:
                    act.wait_ge(pool_added, pool_adds_before(i, False) + POOL_HEADS * (kt - 1) + h + 1)
                else:
                    act.wait_ge(dve_added, DVE_HEADS * ((KT - 1) * i + kt - 1) + h - POOL_HEADS + 1)

            def save(i, y):
                act.wait_ge(pv_done, pv_before(i, y) + KT)
                if y:
                    y_too = not (isinstance(i, int) and i >= images)
                    act.wait_ge(work_full, work_position(i, y_too, "proj0" if y_too else "proj1", 1) + 1)
                elif present(i - 2, images):
                    act.wait_ge(work_full, work_position(i, False, "proj1", 1) + 1)
                act.copy(mix[:, :], acc[:, :]).then_inc(saved, 1)

            def beside(s, par, at, bank):
                name, img, _ = s
                b = int(name[-1])
                name = name[:-1]
                if name in ("q", "k"):
                    which = 0 if name == "q" else 1
                    full = part[2 * which + 1][:, :].bitcast(F32)
                    if b == 1:
                        for h in range(HEADS):
                            act.wait_ge(stacked[h], 16 * STACK_DMAS * (images if isinstance(img, int) and img + 2 > images else img + 2))
                    elif not (isinstance(img, int) and img == 0):
                        for h in range(HEADS):
                            act.wait_ge(stacked[h], 16 * STACK_DMAS * img)
                        if not (isinstance(img, int) and img < 2):
                            act.wait_ge(split_done[1], 2 * (img - 2) + 2)
                elif name == "sums":
                    if b == 0 and not (isinstance(img, int) and img < 2):
                        act.wait_ge(scaled[1], img - 1)
                    if b == 1:
                        both = isinstance(img, int) and img + 2 > images
                        act.wait_ge(scaled[0], images if both else img + 2)
                        if both:
                            act.wait_ge(scaled[1], img)
                elif name == "v":
                    if b == 0 and not (isinstance(img, int) and img < 2):
                        act.wait_ge(pv_done, pv_before(img - 2, False) + KT)
                    if b == 1 and not (isinstance(img, int) and img == 0):
                        act.wait_ge(pv_done, pv_before(img, True) + KT)
                for half in range(2):
                    act.wait_ge(act_full, at + half + 1)
                    src = score[(bank + half) % SCORE_BANKS][:, :]
                    if name in ("q", "k"):
                        bias = vec(b, BQ if which == 0 else BK)
                        act.activation(full[:, halves(half)], src, ACT.Identity, bias=bias).then_inc(act_done, 1)
                    elif name == "v":
                        dst = v0[:, par, :, :] if b == 0 else v1[:, :, :]
                        act.copy(dst[:, 4 * half:4 * half + 4, :].rearrange("p t n -> p (t n)"),
                                 src).then_inc(act_done, 1)
                    else:
                        act.copy(rb[:, halves(half)], src).then_inc(act_done, 1)

            at = 0
            act.wait_ge(const_loaded, 48)
            for s in START:
                if s[0][:-1] in SCORE:
                    beside(s, 0, at, at % SCORE_BANKS)
                    at += 2

            def run(i, parity, y):
                at, bank = scores_before(i, y), scores_before(i if isinstance(i, int) else 2, y) % SCORE_BANKS
                for s in (score_steps_y if y else score_steps_x)(i, images):
                    if s[0][:-1] == "exp":
                        kt, h = s[2]
                        exp(i, parity, y, kt, h, at, bank)
                        if y and kt == 0 and present(i, images):
                            save(i, False)
                        elif not y and (kt, h) == (0, HEADS - 1) and present(i - 2, images):
                            save(i - 1, True)
                    else:
                        beside(s, parity_of(s, parity), at, bank)
                    at, bank = at + 2, (bank + 2) % SCORE_BANKS

            def body(i, parity):
                run(i, parity, False)
                if isinstance(i, int) and i == 0:
                    save(0, False)
                run(i, parity, True)

            bodies(act, body)
            save(images - 1, True)
            run(images, 0, False)
            run(images, 0, True)
            save(images, True)
            run(images + 1, 1, False)

        @block.vector
        def _(dve):
            def group_norm(b, name, img, par, at, bank):
                chain, g, base = gn_chain[b], gn[b], GN_CHAIN * img
                src = xin[:, par, :] if b == 0 else x1[:, par, :]

                def col(n):
                    return g[:, n:n + 1]

                if name == "stats":
                    if b == 0:
                        dve.wait_ge(x_loaded, 16 * (img + 1))
                    else:
                        dve.wait_ge(x1_done, 2 * (img + 1))
                    for h in range(2):
                        dve.bn_stats(stats[b][:, h, :], src[:, halves(h)]).then_inc(chain, 1)
                    dve.wait_ge(chain, base + 2)
                    dve.tensor_copy(col(GAIN), stats[b][:, 0, 0:1])
                    dve.bn_aggr(mv[b][:, :], stats[b][:, :, :]).then_inc(chain, 1)
                elif name == "mean":
                    dve.wait_ge(work_full, at + 1)
                    dve.tensor_tensor(col(DIFF), mv[b][:, 0:1], work[bank][:, 0:1], ALU.subtract).then_inc(chain, 1)
                    dve.tensor_copy(col(GMEAN), work[bank][:, 0:1]).then_inc(work_free, 1)
                    dve.wait_ge(chain, base + 4)
                    dve.scalar_tensor_tensor(out=col(VARIN), in0=col(DIFF), scalar=col(DIFF), in1=mv[b][:, 1:2],
                                             op0=ALU.mult, op1=ALU.add).then_inc(chain, 1)
                elif name == "var":
                    dve.wait_ge(work_full, at + 1)
                    dve.tensor_scalar(col(VAREPS), work[bank][:, 0:1], EPS[b], None, ALU.add).then_inc(chain, 1)
                    dve.wait_ge(chain, base + 6)
                    dve.tensor_copy(col(MG), work[bank][:, 0:1]).then_inc(work_free, 1)
                elif name == "norm":
                    dve.wait_ge(rstd_done[b], img + 1)
                    dve.tensor_tensor(col(GAIN), col(RSTD), vec(b, GAMMA), ALU.mult).then_inc(chain, 1)
                    dve.wait_ge(chain, base + 7)
                    dve.tensor_tensor(col(MG), col(GMEAN), col(GAIN), ALU.mult).then_inc(chain, 1)
                    dve.wait_ge(chain, base + 8)
                    dve.tensor_tensor(col(OFFSET), vec(b, BETA), col(MG), ALU.subtract).then_inc(chain, 1)
                    dve.wait_ge(chain, base + 9)
                    if b == 0 and present(img - 2, images):
                        dve.wait_ge(act_full, score_position(img - 1, False, "v1") + 2)
                    if b == 1 and present(img + 1, images):
                        dve.wait_ge(act_full, score_position(img, False, "v0") + 2)
                    dve.tensor_scalar(xh[:, :], src, col(GAIN), col(OFFSET), ALU.mult, ALU.add).then_inc(chain, 1)

            def split(b, which, img, computed):
                hi, lo = (part, part1)[b][2 * which:2 * which + 2]
                full = part[2 * which + 1][:, :].bitcast(F32)
                dve.wait_ge(act_done, computed + 2)
                if b == 1 and which == 0 and present(img - 1, images):
                    dve.wait_ge(act_full, exp_position(img, True, KT - 1) + 2)
                dve.tensor_copy(hi[:, :], full).then_inc(hi_done[b], 1)
                dve.wait_ge(hi_done[b], 2 * img + which + 1)
                dve.tensor_tensor(lo[:, :], full, hi[:, :].bitcast(F32), ALU.subtract).then_inc(split_done[b], 1)

            def add(i, parity, kt):
                for n, h in enumerate(range(POOL_HEADS, HEADS)):
                    dve.wait_ge(act_done, exp_position(i, False, kt, h) + 2)
                    if kt == 1:
                        dve.wait_ge(pv_done, pv_before(i, False) + 1)
                    else:
                        dve.wait_ge(dve_added, DVE_HEADS * ((KT - 1) * i + kt - 2) + n + 1)
                    dve.tensor_tensor(sum0[:, h, :], sum0[:, h, :],
                                      probs[:, ring_slot(i, parity, False, HEADS * (kt - 1) + h), :],
                                      ALU.add).then_inc(dve_added, 1)

            def step(s, par, at, bank, i, y):
                name, img, arg = s
                b = int(name[-1])
                name = name[:-1]
                if name in ("stats", "mean", "var", "norm"):
                    group_norm(b, name, img, par, at, bank)
                elif name in ("splitq", "splitk"):
                    if i is None:
                        computed = 0 if name == "splitq" else 2
                    else:
                        computed = score_position(i, y, name[-1] + str(b))
                    split(b, 0 if name == "splitq" else 1, img, computed)
                elif name == "add":
                    add(img, par, KT - 1)
                elif name == "max":
                    dve.wait_ge(work_full, at + 1)
                    dve.tensor_reduce(halfmax[b][:, arg // 2, arg % 2:arg % 2 + 1], work[bank][:, :], AX.X,
                                      ALU.max).then_inc(work_free, 1)
                elif name == "gather":
                    dve.wait_ge(work_free, at)
                    dve.tensor_reduce(rowmax[b][:, :], halfmax[b][:, :, :], AX.X, ALU.max).then_inc(rowmax_done[b], 1)
                elif name == "shift":
                    dve.wait_ge(work_full, at + 1)
                    rows = heads_of(b) * KT
                    src = work[bank][0:rows, 0:C]
                    neg_hi, neg_lo = (n[0:rows, :] for n in neg)
                    if b == 1:
                        dve.wait_ge(shift_loaded[0], 32 * (images if isinstance(img, int) and img + 2 > images else img + 2))
                    elif present(img - 2, images):
                        dve.wait_ge(shift_loaded[1], 32 * (img - 1))
                    elif img > 0:
                        dve.wait_ge(shift_loaded[0], 32 * img)
                    dve.tensor_scalar(neg_hi, src, -1.0, None, ALU.mult).then_inc(neg_done[b], 1)
                    dve.wait_ge(neg_done[b], img + 1)
                    dve.scalar_tensor_tensor(out=neg_lo, in0=src, scalar=-1.0, in1=neg_hi.bitcast(F32),
                                             op0=ALU.mult, op1=ALU.subtract).then_inc(work_free, 1)
                elif name == "scale" and on_the_spot(b, img):
                    dve.wait_ge(act_done, score_position(i, y, "sums1") + 2)
                    dve.wait_ge(saved, saved_before(img + 1, True) + 1)
                    for half in range(2):
                        dve.reciprocal(rb[:, halves(half)], rb[:, halves(half)]).then_inc(recip_done[1], 1)
                        dve.wait_ge(recip_done[1], img + half + 1)
                        dve.tensor_tensor(mix[:, halves(half)], mix[:, halves(half)], rb[:, halves(half)],
                                          ALU.mult).then_inc(scaled[1], 1)
                elif name == "recip" and not on_the_spot(b, img):
                    dve.wait_ge(sums_in[b], 16 * (img + 1))
                    dve.reciprocal(compact[b][:, :], compact[b][:, :]).then_inc(recip_done[b], 1)
                elif name == "scale":
                    dve.wait_ge(rb_loaded[b], 16 * heads_of(b) * (img + 1))
                    dve.wait_ge(saved, saved_before(img + b, b == 1) + 1)
                    dve.tensor_tensor(mix[:, :], mix[:, :], rb[:, :], ALU.mult).then_inc(scaled[b], 1)
                elif name == "proj":
                    dve.wait_ge(work_full, at + 1)
                    dst = x1[:, par, halves(arg)]
                    if b == 0 and arg == 0 and present(img - 2, images):
                        dve.wait_ge(stored, 16 * (img - 1))
                    res = xin[:, par, halves(arg)] if b == 0 else dst
                    dve.scalar_tensor_tensor(out=dst, in0=work[bank][:, :], scalar=proj_bias[:, b:b + 1], in1=res,
                                             op0=ALU.add, op1=ALU.add).then_inc(work_free, 1)
                    if b == 0:
                        dve.wait_ge(work_free, at + 1)
                        dve.tensor_scalar(dst, dst, math.sqrt(0.5), None, ALU.mult).then_inc(x1_done, 1)

            dve.wait_ge(const_loaded, 48)
            for b in range(2):
                dve.wait_ge(bias_ready, b + 1)
                dve.tensor_tensor(proj_bias[:, b:b + 1], acc[:, HALF * b:HALF * b + 1], vec(b, BP),
                                  ALU.add).then_inc(bias_added, 1)
            dve.wait_ge(bias_added, 2)

            def run(steps, at, bank, parity, i, y):
                for s in steps:
                    step(s, parity_of(s, parity), at, bank, i, y)
                    if uses_work(s):
                        at, bank = at + 1, (bank + 1) % BANKS
                return at, bank

            run(START, 0, 0, 1, None, False)

            ADD_GAP = 1

            def body(i, parity):
                at, bank = work_before(i, False), first_bank(i, parity)
                for g, steps in enumerate(gaps_x(i, images)):
                    at, bank = run(steps, at, bank, parity, i, False)
                    if g % X_GAPS == ADD_GAP and g // X_GAPS >= 2:
                        add(i, parity, g // X_GAPS - 1)
                for steps in gaps_y(i, images):
                    at, bank = run(steps, at, bank, parity, i, True)

            bodies(dve, body)
            for i in (images, images + 1):
                run(work_steps_x(i, images), work_before(i, False), first_bank(i, i % 2), i % 2, i, False)

        @block.tensor
        def _(pe):
            def work_step(s, par, at, bank):
                name, img, arg = s
                b = int(name[-1])
                name = name[:-1]
                out_bank = work[bank]
                if not (isinstance(at, int) and at < BANKS):
                    pe.wait_ge(work_free, at - BANKS + 1)
                if name == "mean":
                    pe.wait_ge(gn_chain[b], GN_CHAIN * img + 3)
                    mm = pe.matmul(out_bank[:, 0:1], consts[:, 1 + b, :], mv[b][:, 0:1], start=True, stop=True)
                elif name == "var":
                    pe.wait_ge(gn_chain[b], GN_CHAIN * img + 5)
                    mm = pe.matmul(out_bank[:, 0:1], consts[:, 1 + b, :], gn[b][:, VARIN:VARIN + 1], start=True, stop=True)
                elif name == "max":
                    t, half = arg // 2, arg % 2
                    if b == 0:
                        h, t = t // KT, t % KT
                        if t == 0 and half == 0:
                            pe.wait_ge(stacked[h], 16 * STACK_DMAS * (img + 1))
                        mm = pe.matmul(out_bank[:, :], qs[par][0:SPLIT, h, tile(t)], ks[par][0:SPLIT, h, halves(half)],
                                       start=True, stop=True)
                    else:
                        if arg == 0:
                            pe.wait_ge(hi_done[1], 2 * (img + 1))
                        mm = pe.matmul(out_bank[:, :], part1[0][:, tile(t)], part1[2][:, halves(half)], start=True, stop=True)
                elif name == "shift":
                    pe.wait_ge(rowmax_done[b], img + 1)
                    mm = pe.transpose(out_bank[0:heads_of(b) * KT, 0:C], rowmax[b][:, :], identity)
                elif name == "proj":
                    pe.wait_ge(scaled[b], img + 1 + (arg if on_the_spot(b, img) else 0))
                    mm = pe.matmul(out_bank[:, :], w(b, WP), mix[:, halves(arg)], start=True, stop=True)
                mm.then_inc(work_full, 1)

            def free_score_bank(at, bank, half):
                if not (isinstance(at, int) and at + half < SCORE_BANKS):
                    pe.wait_ge(act_done, at + half - SCORE_BANKS + 1)
                return score[(bank + half) % SCORE_BANKS]

            def beside(s, par, at, bank, parts=range(2)):
                name, img, _ = s
                b = int(name[-1])
                name = name[:-1]
                if 0 not in parts:
                    pass
                elif name in ("q", "k", "v"):
                    pe.wait_ge(gn_chain[b], GN_CHAIN * img + 10)
                elif b == 0:
                    pe.wait_ge(pool_added, pool_adds_before(img, False) + (KT - 1) * POOL_HEADS)
                    pe.wait_ge(dve_added, DVE_HEADS * (KT - 1) * (img + 1))
                else:
                    pe.wait_ge(pool_added, pool_adds_before(img + 1, True) + KT - 1)
                for half in parts:
                    dst = free_score_bank(at, bank, half)
                    if name in ("q", "k"):
                        mm = pe.matmul(dst[:, :], w(b, WQ if name == "q" else WK), xh[:, halves(half)], start=True, stop=True)
                    elif name == "v":
                        for t in range(4):
                            mm = pe.matmul(dst[:, tile(t)], xh[:, tile(4 * half + t)], w(b, WV), start=True, stop=True)
                    elif b == 0:
                        for h in range(HEADS):
                            mm = pe.matmul(dst[head(h), :], ones[:, 0:DH].bitcast(F32), sum0[:, h, halves(half)], start=True,
                                           stop=True, tile_position=(0, DH * h))
                    else:
                        mm = pe.matmul(dst[:, :], ones[:, :].bitcast(F32), sum1[:, halves(half)], start=True, stop=True)
                    mm.then_inc(act_full, 1)

            def scores0(i, parity, kt, h, half):
                if kt == 0 and h == 0 and half == 0:
                    pe.wait_ge(shift_loaded[0], 32 * (i + 1))
                at, bank = exp_position(i, False, kt, h), score_bank(i, False, "exp0", (kt, h))
                pe.matmul(free_score_bank(at, bank, half)[:, :], ks[parity][0:SPLIT + SHIFT, h, tile(kt)],
                          qs[parity][0:SPLIT + SHIFT, h, halves(half)], start=True, stop=True).then_inc(act_full, 1)

            def scores1(i, kt, half):
                if kt == 0 and half == 0:
                    pe.wait_ge(shift_loaded[1], 32 * i)
                    pe.wait_ge(split_done[1], 2 * i)
                q_hi, q_lo, k_hi, k_lo = part1
                dst = free_score_bank(exp_position(i, True, kt), score_bank(i, True, "exp1", (kt, 0)), half)[:, :]
                pe.matmul(dst, k_hi[:, tile(kt)], q_hi[:, halves(half)], start=True, stop=False)
                pe.matmul(dst, k_hi[:, tile(kt)], q_lo[:, halves(half)], start=False, stop=False)
                pe.matmul(dst, k_lo[:, tile(kt)], q_hi[:, halves(half)], start=False, stop=False)
                pe.matmul(dst, ones[:, :], shift1[:, halves(half)], start=False, stop=True).then_inc(act_full, 1)

            def pv(i, parity, y, kt, half):
                if half == 0:
                    pe.wait_ge(act_done, exp_position(i, y, kt, 0 if y else HEADS - 1) + 2)
                    if kt == 0 and not (isinstance(i, int) and i == 0):
                        pe.wait_ge(saved, saved_before(i, y))
                for h in range(1 if y else HEADS):
                    if y:
                        dst, v = acc[:, halves(half)], v1[:, kt, :]
                        src = sum1[:, halves(half)] if kt == 0 else probs[:, ring_slot(i, parity, True, kt - 1), halves(half)]
                        where = None
                    else:
                        dst, v = acc[head(h), halves(half)], v0[:, parity, kt, head(h)]
                        src = sum0[:, h, halves(half)] if kt == 0 else \
                            probs[:, ring_slot(i, parity, False, HEADS * (kt - 1) + h), halves(half)]
                        where = (0, DH * h)
                    mm = pe.matmul(dst, v, src, start=kt == 0, stop=kt == KT - 1, tile_position=where)
                if half == 1:
                    mm.then_inc(pv_done, 1)

            pe.wait_ge(const_loaded, 48)
            for b in range(2):
                pe.matmul(acc[:, HALF * b:HALF * b + 1], w(b, WP), vec(b, BV), start=True, stop=True).then_inc(bias_ready, 1)
            pe.wait_ge(bias_added, 2)
            pe.wait_ge(pool_ready, 5)

            def run(steps, at, bank, parity):
                for s in steps:
                    if uses_work(s):
                        work_step(s, parity_of(s, parity), at, bank)
                        at, bank = at + 1, (bank + 1) % BANKS
                return at, bank

            at, bank, score_at = 0, 0, 0
            for s in START:
                if s[0][:-1] in SCORE:
                    beside(s, 0, score_at, score_at % SCORE_BANKS)
                    score_at += 2
                else:
                    at, bank = run([s], at, bank, 1)

            def beside_after(table, n, i, parity, y, parts=range(2)):
                for name, ahead, at in table:
                    if at == n and present(i + ahead, images):
                        s = (name, i + ahead, None)
                        beside(s, parity_of(s, parity), score_position(i, y, name), score_bank(i, y, name), parts)

            def body_x(i, parity, at, bank):
                gaps = gaps_x(i, images)
                for kt in range(KT):
                    if kt:
                        before = (i, parity, False, kt - 1)
                    elif present(i - 2, images):
                        before = (i - 1, 1 - parity, True, KT - 1)
                    else:
                        before = None
                    own = gaps[X_GAPS * kt:X_GAPS * (kt + 1)]
                    for h in range(HEADS):
                        scores0(i, parity, kt, h, 0)
                        if h % 2 == 0:
                            at, bank = run(own.pop(0), at, bank, parity)
                        elif before:
                            pv(*before, h // 2)
                        scores0(i, parity, kt, h, 1)
                        beside_after(BESIDE_X, HEADS * kt + h, i, parity, False, (0,))
                        at, bank = run(own.pop(0), at, bank, parity)
                        beside_after(BESIDE_X, HEADS * kt + h, i, parity, False, (1,))
                return at, bank

            def body_y(i, parity, at, bank):
                gaps = gaps_y(i, images)
                for kt in range(KT):
                    own = gaps[Y_GAPS * kt:Y_GAPS * (kt + 1)]
                    if kt:
                        before = (i, parity, True, kt - 1)
                    else:
                        before = (i, parity, False, KT - 1) if present(i, images) else None
                    for half in range(2):
                        if present(i - 1, images):
                            scores1(i, kt, half)
                        at, bank = run(own.pop(0), at, bank, parity)
                    beside_after(BESIDE_Y, kt, i, parity, True)
                    for half in range(2):
                        if before and (present(i - 1, images) or kt == 0):
                            pv(*before, half)
                        at, bank = run(own.pop(0), at, bank, parity)
                return at, bank

            def body(i, parity):
                body_y(i, parity, *body_x(i, parity, work_before(i, False), first_bank(i, parity)))

            bodies(pe, body)
            for half in range(2):
                pv(images - 1, 1, True, KT - 1, half)
            for n in range(KT * HEADS):
                beside_after(BESIDE_X, n, images, 0, False)
            run(work_steps_x(images, images), work_before(images, False), first_bank(images, 0), 0)
            body_y(images, 0, work_before(images, True), 0)
            for half in range(2):
                pv(images, 0, True, KT - 1, half)
            for n in range(KT * HEADS):
                beside_after(BESIDE_X, n, images + 1, 1, False)
            run(work_steps_x(images + 1, images), work_before(images + 1, False), first_bank(images + 1, 1), 1)


def kernel(**inputs):
    import numpy as np
    import concourse.bacc as bacc
    from concourse.bass_utils import run_bass_kernel_spmd as run

    a = {k: np.ascontiguousarray(v) for k, v in inputs.items()}
    wq1, wk1, wv1 = a["L1_conv_qkv_w"].reshape(3, C, C)
    weights = np.ascontiguousarray(np.stack(
        [a["L0_conv_Wq"], a["L0_conv_Wk"], a["L0_conv_Wv"], a["L0_conv_Wp"],
         wq1.T, wk1.T, wv1.T, a["L1_conv_proj_w"].T], axis=1))
    bq1, bk1, bv1 = a["L1_conv_qkv_b"].reshape(3, C)
    vectors = np.ascontiguousarray(np.stack(
        [a["L0_conv_gn_scale"], a["L0_conv_gn_bias"], a["L0_conv_bq"], a["L0_conv_bk"], a["L0_conv_bv"],
         a["L0_conv_bp"], a["L1_conv_gn_w"], a["L1_conv_gn_b"], bq1, bk1, bv1, a["L1_conv_proj_b"]], axis=1))
    channel = np.arange(C)
    constants = np.stack(
        [np.eye(C)] + [(channel[:, None] // g == channel[None, :] // g) / g for g in (C // 32, C // 8)],
        axis=1).astype(np.float32)
    arrays = {"x_dram": a["x"], "weights_dram": weights, "vectors_dram": vectors,
              "constants_dram": np.ascontiguousarray(constants)}

    nc = bacc.Bacc("TRN2", target_bir_lowering=False, num_devices=1)
    args = [nc.dram_tensor(n, v.shape, mybir.dt.from_np(v.dtype), kind="ExternalInput").ap() for n, v in arrays.items()]
    out = nc.dram_tensor("out_0_dram", a["x"].shape, F32, kind="ExternalOutput").ap()
    bass_two_attention_blocks(nc, *args, out)
    return run(nc, [arrays], core_ids=[0]).results[0]["out_0_dram"]
```
